# Optimizing a Trainium2 kernel written in Bass

```python
import numpy as np
import jax
import jax.numpy as jnp

def _softmax(x, axis=-1):
    return jax.nn.softmax(x, axis=axis)

def _gelu(x):
    return jax.nn.gelu(x, approximate=True)

def _silu(x):
    return jax.nn.silu(x)

def _sigmoid(x):
    return jax.nn.sigmoid(x)

def _layernorm(x, axis=-1, eps=1e-05):
    m = jnp.mean(x, axis=axis, keepdims=True)
    v = jnp.var(x, axis=axis, keepdims=True)
    return (x - m) / jnp.sqrt(v + eps)

def _scatter_add(tgt, idx, src, axis=0):
    return tgt.at[idx].add(src)

def _segment_sum(src, seg, n):
    return jax.ops.segment_sum(src, seg, n)
kernel_name = 'mk_gnn_ffn_d1_gnn_r64_582a8c'

def setup_inputs(seed: int=0):
    np.random.seed(seed)
    _w = jnp.asarray

    def _rec_inputs():
        import jax
        import jax.numpy as jnp
        _gk = jax.random.key(seed)
        x = -0.0003713 + 1 * jax.random.normal(jax.random.fold_in(_gk, 1), (50000, 256), jnp.float32)
        src = jax.random.randint(jax.random.fold_in(_gk, 2), (12500,), 0, 50000, jnp.int32)
        dst = jax.random.randint(jax.random.fold_in(_gk, 3), (12500,), 0, 50000, jnp.int32)
        _o = jnp.argsort(dst, stable=True)
        src = src[_o]
        dst = dst[_o]
        return (x, src, dst)
    x, src, dst = _rec_inputs()

    def _L0_gnn_setup():
        import jax, jax.numpy as jnp
        import numpy as np
        N_NODES = 50000
        EPS = 1e-12
        key = jax.random.key(seed)
        k1, k2, k3 = jax.random.split(key, 3)
        d_in, d_out, n_edges = (256, 256, 12500)
        input_matrix = jax.random.normal(k1, (N_NODES, d_in), dtype=jnp.float32)
        adjacency_coo_matrix = jax.random.randint(k2, (2, n_edges), 0, N_NODES, dtype=jnp.int64)
        W = jax.random.normal(k3, (2 * d_in, d_out), dtype=jnp.float32) * (1.0 / np.sqrt(2 * d_in))
        b = jnp.zeros((d_out,), dtype=jnp.float32)
        return {'input_matrix': input_matrix, 'adjacency_coo_matrix': adjacency_coo_matrix, 'W': W, 'b': b}
    _L0_gnn_all = _L0_gnn_setup()
    _L0_gnn_in = {k: v for k, v in _L0_gnn_all.items() if k in ('W', 'b')}
    del _L0_gnn_all

    def _L0_ffn_setup():
        import jax, jax.numpy as jnp
        import numpy as np
        DIM = 256
        H = 8
        D = 64
        G = 64
        INNER = H * D
        SCALE = D ** (-0.5)
        key = jax.random.key(seed)
        ks = jax.random.split(key, 12)
        B, N = (4, 256)
        x = jax.random.normal(ks[0], (B, N, DIM), dtype=jnp.float32)
        s = lambda fan_in: 1.0 / np.sqrt(fan_in)
        W_fx = jax.random.normal(ks[1], (DIM, INNER), dtype=jnp.float32) * s(DIM)
        b_fx = jnp.zeros((INNER,), dtype=jnp.float32)
        W_x = jax.random.normal(ks[2], (DIM, INNER), dtype=jnp.float32) * s(DIM)
        b_x = jnp.zeros((INNER,), dtype=jnp.float32)
        A = jax.random.normal(ks[3], (G, D), dtype=jnp.float32)
        Q, _ = jnp.linalg.qr(A.T)
        W_slice = Q[:, :G].astype(jnp.float32)
        b_slice = jnp.zeros((G,), dtype=jnp.float32)
        W_q = jax.random.normal(ks[4], (D, D), dtype=jnp.float32) * s(D)
        W_k = jax.random.normal(ks[5], (D, D), dtype=jnp.float32) * s(D)
        W_v = jax.random.normal(ks[6], (D, D), dtype=jnp.float32) * s(D)
        W_out = jax.random.normal(ks[7], (INNER, DIM), dtype=jnp.float32) * s(INNER)
        b_out = jnp.zeros((DIM,), dtype=jnp.float32)
        temperature = jnp.ones((1, H, 1, 1), dtype=jnp.float32) * 0.5
        return {'x': x, 'W_fx': W_fx, 'b_fx': b_fx, 'W_x': W_x, 'b_x': b_x, 'W_slice': W_slice, 'b_slice': b_slice, 'W_q': W_q, 'W_k': W_k, 'W_v': W_v, 'W_out': W_out, 'b_out': b_out, 'temperature': temperature}
    _L0_ffn_all = _L0_ffn_setup()
    _L0_ffn_in = {k: v for k, v in _L0_ffn_all.items() if k in ('W_fx', 'b_fx', 'W_x', 'b_x', 'W_slice', 'b_slice', 'W_q', 'W_k', 'W_v', 'W_out', 'b_out', 'temperature')}
    del _L0_ffn_all
    return {'x': x, 'src': src, 'dst': dst, 'L0_gnn_W': _L0_gnn_in['W'], 'L0_gnn_b': _L0_gnn_in['b'], 'L0_ffn_W_fx': _L0_ffn_in['W_fx'], 'L0_ffn_b_fx': _L0_ffn_in['b_fx'], 'L0_ffn_W_x': _L0_ffn_in['W_x'], 'L0_ffn_b_x': _L0_ffn_in['b_x'], 'L0_ffn_W_slice': _L0_ffn_in['W_slice'], 'L0_ffn_b_slice': _L0_ffn_in['b_slice'], 'L0_ffn_W_q': _L0_ffn_in['W_q'], 'L0_ffn_W_k': _L0_ffn_in['W_k'], 'L0_ffn_W_v': _L0_ffn_in['W_v'], 'L0_ffn_W_out': _L0_ffn_in['W_out'], 'L0_ffn_b_out': _L0_ffn_in['b_out'], 'L0_ffn_temperature': _L0_ffn_in['temperature']}

def reference(x, src, dst, L0_gnn_W, L0_gnn_b, L0_ffn_W_fx, L0_ffn_b_fx, L0_ffn_W_x, L0_ffn_b_x, L0_ffn_W_slice, L0_ffn_b_slice, L0_ffn_W_q, L0_ffn_W_k, L0_ffn_W_v, L0_ffn_W_out, L0_ffn_b_out, L0_ffn_temperature):
    import jax
    import jax.numpy as jnp

    def _L0_gnn_ref(input_matrix, adjacency_coo_matrix, W, b):
        import jax, jax.numpy as jnp
        import numpy as np
        N_NODES = 50000
        EPS = 1e-12
        src = adjacency_coo_matrix[0]
        dst = adjacency_coo_matrix[1]
        neigh_sum = jax.ops.segment_sum(input_matrix[src], dst, num_segments=N_NODES)
        deg = jax.ops.segment_sum(jnp.ones_like(dst, dtype=input_matrix.dtype), dst, num_segments=N_NODES)
        neigh_mean = neigh_sum / jnp.maximum(deg, 1.0)[:, None]
        h = jnp.concatenate([input_matrix, neigh_mean], axis=-1)
        out = jax.nn.relu(h @ W + b)
        norm = jnp.maximum(jnp.linalg.norm(out, axis=-1, keepdims=True), EPS)
        return out / norm

    def _L0_ffn_ref(x, W_fx, b_fx, W_x, b_x, W_slice, b_slice, W_q, W_k, W_v, W_out, b_out, temperature):
        import jax, jax.numpy as jnp
        import numpy as np
        DIM = 256
        H = 8
        D = 64
        G = 64
        INNER = H * D
        SCALE = D ** (-0.5)
        B, N, _ = x.shape
        fx_mid = (x @ W_fx + b_fx).reshape(B, N, H, D).transpose(0, 2, 1, 3)
        x_mid = (x @ W_x + b_x).reshape(B, N, H, D).transpose(0, 2, 1, 3)
        temp = jnp.clip(temperature, 0.1, 5.0)
        slice_weights = jax.nn.softmax((x_mid @ W_slice + b_slice) / temp, axis=-1)
        slice_norm = slice_weights.sum(axis=2)
        slice_token = jnp.einsum('bhnc,bhng->bhgc', fx_mid, slice_weights)
        slice_token = slice_token / (slice_norm[..., None] + 1e-05)
        q = slice_token @ W_q
        k = slice_token @ W_k
        v = slice_token @ W_v
        attn = jax.nn.softmax(jnp.einsum('bhgc,bhkc->bhgk', q, k) * SCALE, axis=-1)
        out_slice = jnp.einsum('bhgk,bhkc->bhgc', attn, v)
        out_x = jnp.einsum('bhgc,bhng->bhnc', out_slice, slice_weights)
        out_x = out_x.transpose(0, 2, 1, 3).reshape(B, N, INNER)
        return out_x @ W_out + b_out
    edge_index = jnp.stack([src, dst])
    x = x + _L0_gnn_ref(_layernorm(x, axis=-1), edge_index, L0_gnn_W, L0_gnn_b)
    x = x + _L0_ffn_ref(_layernorm(x, axis=-1)[None], L0_ffn_W_fx, L0_ffn_b_fx, L0_ffn_W_x, L0_ffn_b_x, L0_ffn_W_slice, L0_ffn_b_slice, L0_ffn_W_q, L0_ffn_W_k, L0_ffn_W_v, L0_ffn_W_out, L0_ffn_b_out, L0_ffn_temperature)[0]
    return x

_drawn_inputs = setup_inputs


def setup_inputs(seed=0):
    import zlib

    import numpy as np

    out = dict(_drawn_inputs(seed))
    spreads = {'L0_gnn_b': (0.0, 0.8),
     'L0_ffn_b_fx': (0.0, 0.1),
     'L0_ffn_b_x': (0.0, 0.8),
     'L0_ffn_b_slice': (0.0, 0.8),
     'L0_ffn_b_out': (0.0, 0.1),
     'L0_ffn_temperature': (0.5, 0.6)}
    factors = {'L0_ffn_W_fx': 7.009,
     'L0_ffn_W_x': 8.0,
     'L0_ffn_W_slice': 8.0,
     'L0_ffn_W_q': 8.0,
     'L0_ffn_W_k': 8.0}
    for name, (base, spread) in spreads.items():
        noise = np.random.default_rng([zlib.crc32(name.encode()), seed]).standard_normal(out[name].shape)
        drawn = base * np.exp(spread * noise) if base else spread * noise
        out[name] = jnp.asarray(drawn.astype(out[name].dtype))
    for name, factor in factors.items():
        out[name] = (out[name] * factor).astype(out[name].dtype)
    return out
```

```python
from contextlib import ExitStack

import concourse.bass as bass
from concourse import mybir

F32 = mybir.dt.float32
F32R = mybir.dt.float32r
BF16 = mybir.dt.bfloat16
I32 = mybir.dt.int32
ALU = mybir.AluOpType
ACT = mybir.ActivationFunctionType
AX = mybir.AxisListType.X

P = 128
D = 256
NODES = 50000
EDGES = 12500
HEADS, HD, SLICES = 8, 64, 64
HG = HEADS * SLICES
KC = D // P
HC = HG // P

TILES = 4
GROUP = P * TILES
GROUPS = -(-NODES // GROUP)
LAST_ROWS = (NODES - (GROUPS - 1) * GROUP) // TILES
assert (NODES - (GROUPS - 1) * GROUP) % TILES == 0
PAIRS = GROUPS * 2

CHUNKS = -(-EDGES // P)
SLOTS = CHUNKS * P
TAIL_EDGES = EDGES - (CHUNKS - 1) * P
NO_NODE = 1 << 17
SKIP = 1 << 20

LN_EPS = 1e-5
NORM_EPS = 1e-12
SCALE = HD ** -0.5


def at_least(engine, sem, value):
    if not isinstance(value, int) or value > 0:
        engine.wait_ge(sem, value)


def run_steps(engine, items, lag, unroll, peel, step):
    full = items // unroll
    for s in range(peel * unroll):
        step(s // unroll, s % unroll)
    with engine.Fori(peel, full) as turn:
        for j in range(unroll):
            step(turn, j)
    for s in range(full * unroll, items + lag):
        step(s // unroll, s % unroll)


def inside(n, total):
    return not isinstance(n, int) or 0 <= n < total


def row(view, n):
    return view[bass.ds(n, 1)].rearrange("a p d -> (a p) d")


def build(nc, x, src, dst, gW, gb, W_fx, b_fx, W_x, b_x, W_slice, b_slice, W_q, W_k, W_v, W_out, b_out,
          temperature, out):
    with ExitStack() as ctx:
        def sb(name, shape, dt=F32, stack=ctx):
            return stack.enter_context(nc.sbuf_tensor(name, shape, dt))

        def sem(name):
            return ctx.enter_context(nc.semaphore(name))

        gated = {nc.gpsimd: sem("pool_gates"), nc.vector: sem("vector_gates")}

        def gate(engine):
            engine.sem_inc(gated[engine], 1)

        ctx.enter_context(nc.allow_non_contiguous_dma("broadcast rows of the small weights"))
        bank = [ctx.enter_context(nc.psum_tensor(f"bank{i}", [P, 512], F32)) for i in range(8)]

        e_src = nc.dram_tensor("e_src", (SLOTS, 1), I32).ap()
        e_dst = nc.dram_tensor("e_dst", (SLOTS + P, 1), I32).ap()
        nbr = nc.dram_tensor("nbr", (GROUPS * GROUP, D), F32).ap()
        x1_s = nc.dram_tensor("x1_s", (GROUPS * GROUP, D), F32).ap()
        wT_s = nc.dram_tensor("wT_s", (PAIRS, P, 2 * HG), F32).ap()

        full = (GROUPS - 1) * GROUP
        x_g = x[0:full].rearrange("(g p j) d -> g p (j d)", p=P, j=TILES)
        x_last = x[full:NODES].rearrange("(p j) d -> p (j d)", j=TILES)
        out_g = out[0:full].rearrange("(g p j) d -> g p (j d)", p=P, j=TILES)
        out_last = out[full:NODES].rearrange("(p j) d -> p (j d)", j=TILES)
        nbr_g = nbr.rearrange("(g p j) d -> g p (j d)", p=P, j=TILES)
        x1_g = x1_s.rearrange("(g p j) d -> g p (j d)", p=P, j=TILES)

        ident = sb("ident", [P, P])
        ident_r = sb("ident_r", [P, P], F32R)
        ones_bf = sb("ones_bf", [P, P], BF16)
        W1H = sb("W1H", [P, KC, D], F32R)
        W1L = sb("W1L", [P, KC, D], F32R)
        W2 = sb("W2", [P, KC, D])
        CH = sb("CH", [P, KC, HG], F32R)
        CL = sb("CL", [P, KC, HG], F32R)
        bias_z = sb("bias_z", [P, D], BF16)
        bias_l = sb("bias_l", [P, HG], BF16)
        bias_o = sb("bias_o", [P, D], BF16)
        WfxA = sb("WfxA", [P, KC, HG])
        wq = sb("wq", [HD, HD])
        wk = sb("wk", [HD, HD])
        wv = sb("wv", [HD, HD])
        wo = sb("wo", [HD, HEADS, D])
        pick_last = sb("pick_last", [P, P])
        last_row = sb("last_row", [P, 1])
        minus_half = sb("minus_half", [P, 4])
        key_col = sb("key_col", [P, CHUNKS])
        src_i = sb("src_i", [P, CHUNKS], I32)
        tgt_i = sb("tgt_i", [P, CHUNKS], I32)

        with ExitStack() as stage:
            PIECE = SLOTS // 4
            w1 = sb("w1", [P, KC, D], stack=stage)
            wx = sb("wx", [P, KC, HG], stack=stage)
            wxT = sb("wxT", [HD, HEADS, D], stack=stage)
            ws = sb("ws", [HD, SLICES], stack=stage)
            bxT = sb("bxT", [HD, HEADS], stack=stage)
            bs = sb("bs", [P, SLICES], stack=stage)
            tinv = sb("tinv", [P, HEADS], stack=stage)
            tclip = sb("tclip", [P, HEADS], stack=stage)
            c_f = sb("c_f", [P, KC, HG], stack=stage)
            bz_f = sb("bz_f", [P, D], stack=stage)
            bl_f = sb("bl_f", [P, HG], stack=stage)
            bo_f = sb("bo_f", [P, D], stack=stage)
            part = sb("part", [P, 3, HG], BF16, stack=stage)
            rest = sb("rest", [P, 2, HG], stack=stage)
            acc = sb("acc", [P, 2, HG], stack=stage)
            wfx_mid = sb("wfx_mid", [P, HG], stack=stage)
            dst_r = sb("dst_r", [CHUNKS, P], I32, stack=stage)
            nxt_r = sb("nxt_r", [CHUNKS, P], I32, stack=stage)
            src_r = sb("src_r", [CHUNKS, P], I32, stack=stage)
            rows_f = sb("rows_f", [CHUNKS, 3, P], stack=stage)
            down = sb("down", [CHUNKS, P], stack=stage)
            down_c = sb("down_c", [CHUNKS, 1], stack=stage)
            flag_f = sb("flag_f", [1, 1], stack=stage)
            flag = sb("flag", [1, 1], I32, stack=stage)
            raw = sb("raw", [P, 2, CHUNKS], stack=stage)
            nxt_c = sb("nxt_c", [P, CHUNKS], stack=stage)
            same = sb("same", [P, CHUNKS], stack=stage)
            tgt_f = sb("tgt_f", [P, CHUNKS], stack=stage)
            all_i = sb("all_i", [P, PIECE], I32, stack=stage)
            all_f = sb("all_f", [P, 4, PIECE], stack=stage)
            place = sb("place", [P, PIECE], stack=stage)
            before = sb("before", [P, PIECE], stack=stage)
            edge_id = sb("edge_id", [P, 4, CHUNKS], stack=stage)
            rank4 = sb("rank4", [P, 4], stack=stage)
            rank_f = sb("rank_f", [P, 1], stack=stage)
            rank_i = sb("rank_i", [P, 1], I32, stack=stage)
            spare = sb("spare", [P, 1], stack=stage)
            moved = sb("moved", [P, 2], I32, stack=stage)
            small = sem("small_weights_in")
            big = sem("big_weights_in")
            bfx_in = sem("bfx_in")
            edges_in = sem("edges_in")
            filled = sem("pads_filled")
            kept = sem("edges_kept")
            again = sem("sorted_edges_in")
            consts = sem("constants_set")
            selected = sem("constants_selected")
            wx_turned = sem("wx_turned")
            wx_copied = sem("wx_copied")
            c_done = sem("c_done")
            c_scaled = sem("c_scaled")
            step = sem("vector_step")
            fx_sub = sem("wfx_less_middle")
            down_ready = sem("down_ready")
            down_turned = sem("down_turned")
            flag_ready = sem("flag_ready")
            raw_rows = sem("raw_rows")
            raw_turned = sem("raw_turned")
            raw_ready = sem("raw_columns")
            sorted_rows = sem("sorted_rows")
            sorted_turned = sem("sorted_turned")
            order_done = sem("order_done")
            all_in = sem("all_dst_in")
            ranked = sem("ranked")
            scattered = sem("scattered")
            fall_iota = sem("places_set")
            counted = sem("rank_steps")
            chunks_scattered = sem("chunks_scattered")

            block = stage.enter_context(nc.Block())

            @block.sync
            def _(sp):
                def edge_rows(tile, source, shift, done):
                    whole = (CHUNKS - 1) * P
                    sp.dma_start(tile[0:CHUNKS - 1, :],
                                 source[shift:whole + shift].rearrange("(c i) -> c i", i=P)).then_inc(done, 16)
                    sp.dma_start(tile[CHUNKS - 1:CHUNKS, 0:TAIL_EDGES - shift],
                                 source[whole + shift:EDGES].rearrange("(c i) -> c i", c=1)).then_inc(done, 16)

                sp.wait_ge(filled, 3)
                edge_rows(dst_r, dst, 0, edges_in)
                edge_rows(nxt_r, dst, 1, edges_in)
                edge_rows(src_r, src, 0, edges_in)
                sp.dma_start(wx[:, :, :], W_x.rearrange("(k p) n -> p k n", p=P)).then_inc(big, 16)
                sp.dma_start(w1[:, :, :], gW[0:D].rearrange("(k p) n -> p k n", p=P)).then_inc(big, 16)
                sp.dma_start(W2[:, :, :], gW[D:2 * D].rearrange("(k p) n -> p k n", p=P)).then_inc(big, 16)
                sp.wait_ge(edges_in, 6 * 16)
                by_chunk = e_dst[0:SLOTS].rearrange("(c i) a -> c (i a)", i=P)
                sp.dma_start(by_chunk, dst_r[:, :]).then_inc(kept, 16)
                sp.dma_start(e_src.rearrange("(c i) a -> c (i a)", i=P), src_r[:, :]).then_inc(kept, 16)
                sp.dma_start(e_dst[SLOTS:SLOTS + P - TAIL_EDGES].rearrange("(c i) a -> c (i a)", c=1),
                             dst_r[CHUNKS - 1:CHUNKS, TAIL_EDGES:P]).then_inc(kept, 16)
                sp.wait_ge(order_done, 1)
                sp.wait_ge(raw_ready, 1)
                sp.dma_start(dst_r[:, :], by_chunk).then_inc(again, 16)
                sp.dma_start(nxt_r[:, :], e_dst[1:SLOTS + 1].rearrange("(c i) a -> c (i a)", i=P)).then_inc(again, 16)
                sp.dma_start(src_r[:, :], e_src.rearrange("(c i) a -> c (i a)", i=P)).then_inc(again, 16)
                sp.wait_ge(again, 3 * 16)

            @block.scalar
            def _(act):
                act.dma_start(ws[:, :], W_slice).then_inc(small, 16)
                act.dma_start(bxT[:, :], b_x.rearrange("(h d) -> d h", d=HD)).then_inc(small, 16)
                act.dma_start(bs[:, :], b_slice.partition_broadcast(P)).then_inc(small, 16)
                act.dma_start(tinv[:, :], temperature.rearrange("a h b c -> (a h b c)").partition_broadcast(P)).then_inc(small, 16)
                act.dma_start(bz_f[:, :], gb.partition_broadcast(P)).then_inc(small, 16)
                act.dma_start(bo_f[:, :], b_out.partition_broadcast(P)).then_inc(small, 16)
                act.dma_start(WfxA[:, 0, :], W_fx[0:P]).then_inc(small, 16)
                act.dma_start(WfxA[0:P - 1, 1, :], W_fx[P + 1:D]).then_inc(small, 16)
                act.dma_start(WfxA[P - 1:P, 1, :], b_fx.rearrange("(a n) -> a n", a=1)).then_inc(small, 16)
                act.dma_start(wfx_mid[:, :], W_fx[P:P + 1].rearrange("a n -> (a n)").partition_broadcast(P)).then_inc(small, 16)
                act.dma_start(wq[:, :], W_q).then_inc(small, 16)
                act.dma_start(wk[:, :], W_k).then_inc(small, 16)
                act.dma_start(wv[:, :], W_v).then_inc(small, 16)
                act.dma_start(wo[:, :, :], W_out.rearrange("(h d) n -> d h n", d=HD)).then_inc(small, 16)
                for q in range(4):
                    act.wait_ge(wx_turned, q + 1)
                    act.activation(wxT[:, 2 * q:2 * q + 2, :].rearrange("d h c -> d (h c)"), bank[q][0:HD, :],
                                   ACT.Copy).then_inc(wx_copied, 1)
                act.wait_ge(fx_sub, 2)
                act.dma_start(WfxA[P - 1:P, 1, :], b_fx.rearrange("(a n) -> a n", a=1)).then_inc(bfx_in, 16)
                act.wait_ge(small, 14 * 16)
                act.wait_ge(bfx_in, 16)

            @block.gpsimd
            def _(pool):
                pool.memset(dst_r[:, :], NO_NODE).then_inc(filled, 1)
                pool.memset(nxt_r[:, :], NO_NODE).then_inc(filled, 1)
                pool.memset(src_r[:, :], 0).then_inc(filled, 1)
                pool.memset(ident[:, :], 0.0).then_inc(consts, 1)
                pool.memset(pick_last[:, :], 0.0).then_inc(consts, 1)
                pool.memset(last_row[:, :], 0.0).then_inc(consts, 1)
                pool.memset(ones_bf[:, :], 1.0).then_inc(consts, 1)
                pool.memset(minus_half[:, :], -0.5).then_inc(consts, 1)
                pool.wait_ge(consts, 5)
                pool.affine_select(out=ident[:, :], in_=ident[:, :], compare_op=ALU.not_equal, fill=1.0,
                                   base=0, pattern=[[-1, P]], channel_multiplier=1).then_inc(selected, 1)
                pool.affine_select(out=pick_last[:, :], in_=pick_last[:, :], compare_op=ALU.not_equal, fill=1.0,
                                   base=1 - P, pattern=[[0, P]], channel_multiplier=1).then_inc(selected, 1)
                pool.affine_select(out=last_row[:, :], in_=last_row[:, :], compare_op=ALU.not_equal, fill=1.0,
                                   base=1 - P, pattern=[[0, 1]], channel_multiplier=1).then_inc(selected, 1)
                pool.wait_ge(kept, 3 * 16)
                pool.wait_ge(flag_ready, 1)
                unsorted = pool.value_load(flag[0:1, 0:1], min_val=0, max_val=1)
                with pool.If(unsorted > 0):
                    pool.iota(before[:, :], [[1, PIECE]], base=0, channel_multiplier=0,
                              allow_small_or_imprecise_dtypes=True).then_inc(fall_iota, 1)
                    for q in range(4):
                        pool.iota(edge_id[:, q, :], [[P, CHUNKS]], base=-q * PIECE, channel_multiplier=1,
                                  allow_small_or_imprecise_dtypes=True).then_inc(fall_iota, 1)
                    for q in range(4):
                        pool.dma_start(all_i[:, :], e_dst[q * PIECE:(q + 1) * PIECE].rearrange("n a -> (n a)").partition_broadcast(P)).then_inc(all_in, 16)
                        pool.wait_ge(ranked, q + 1)
                    pool.memset(spare[:, :], 0.0).then_inc(chunks_scattered, 1)
                    with pool.Fori(0, CHUNKS) as c:
                        pool.wait_ge(ranked, c + 5)
                        gate(pool)
                        pool.indirect_dma_start(e_dst[0:SLOTS, :], bass.IndirectOffsetOnAxis(ap=rank_i[:, 0:1], axis=0),
                                                moved[:, 0:1], None).then_inc(scattered, 16)
                        pool.indirect_dma_start(e_src, bass.IndirectOffsetOnAxis(ap=rank_i[:, 0:1], axis=0),
                                                moved[:, 1:2], None).then_inc(scattered, 16)
                        pool.wait_ge(scattered, c * 32 + 32)
                        gate(pool)
                        pool.memset(spare[:, :], 0.0).then_inc(chunks_scattered, 1)
                pool.memset(spare[:, :], 0.0).then_inc(order_done, 1)

            @block.vector
            def _(v):
                done = [0]

                def then(instruction):
                    instruction.then_inc(step, 1)
                    done[0] += 1
                    v.wait_ge(step, done[0])

                v.wait_ge(edges_in, 6 * 16)
                v.tensor_copy(rows_f[:, 0, :], dst_r[:, :])
                v.tensor_copy(rows_f[:, 1, :], src_r[:, :]).then_inc(raw_rows, 1)
                then(v.tensor_copy(rows_f[:, 2, :], nxt_r[:, :]))
                then(v.tensor_tensor(down[:, :], rows_f[:, 2, :], rows_f[:, 0, :], ALU.is_lt))
                v.reduce_max(down_c[:, :], down[:, :], AX).then_inc(down_ready, 1)
                v.wait_ge(down_turned, 1)
                then(v.reduce_max(flag_f[:, :], bank[7][0:1, 0:CHUNKS], AX))
                v.tensor_copy(flag[:, :], flag_f[:, :]).then_inc(flag_ready, 1)
                v.wait_ge(raw_turned, 1)
                v.tensor_copy(raw[:, 0, :], bank[4][:, 0:CHUNKS]).then_inc(raw_ready, 1)
                then(v.tensor_copy(raw[:, 1, :], bank[4][:, P:P + CHUNKS]))
                v.wait_ge(flag_ready, 1)
                unsorted = v.value_load(flag[0:1, 0:1], min_val=0, max_val=1)
                with v.If(unsorted > 0):
                    for q in range(4):
                        v.wait_ge(all_in, 16 * (q + 1))
                        v.tensor_copy(all_f[:, q, :], all_i[:, :]).then_inc(ranked, 1)
                    v.wait_ge(fall_iota, 5)
                    v.wait_ge(ranked, 4)
                    with v.Fori(0, CHUNKS) as c:
                        for q in range(4):
                            v.tensor_scalar(place[:, :], before[:, :], edge_id[:, q, bass.ds(c, 1)], -0.5,
                                            ALU.is_lt, ALU.mult).then_inc(counted, 1)
                            v.wait_ge(counted, c * 13 + 3 * q + 1)
                            v.tensor_tensor(place[:, :], place[:, :], all_f[:, q, :], ALU.add).then_inc(counted, 1)
                            v.wait_ge(counted, c * 13 + 3 * q + 2)
                            v.tensor_scalar(place[:, :], place[:, :], raw[:, 0, bass.ds(c, 1)], 0.0,
                                            ALU.is_lt, ALU.add, accum_out=rank4[:, q:q + 1]).then_inc(counted, 1)
                            v.wait_ge(counted, c * 13 + 3 * q + 3)
                        v.reduce_sum(rank_f[:, :], rank4[:, :], AX).then_inc(counted, 1)
                        v.wait_ge(counted, c * 13 + 13)
                        v.wait_ge(chunks_scattered, c + 1)
                        gate(v)
                        v.tensor_copy(moved[:, 0:1], raw[:, 0, bass.ds(c, 1)])
                        v.tensor_copy(moved[:, 1:2], raw[:, 1, bass.ds(c, 1)])
                        v.tensor_copy(rank_i[:, :], rank_f[:, :]).then_inc(ranked, 1)

                v.wait_ge(small, 14 * 16)
                v.wait_ge(selected, 3)
                v.tensor_copy(ident_r[:, :], ident[:, :])
                then(v.tensor_scalar(tclip[:, :], tinv[:, :], 0.1, 5.0, ALU.max, ALU.min))
                then(v.reciprocal(tinv[:, :], tclip[:, :]))
                over_slices = tinv[:, :].unsqueeze(2).to_broadcast([P, HEADS, SLICES])
                v.wait_ge(c_done, 1)
                for k in range(KC):
                    then(v.tensor_tensor(c_f[:, k, :].rearrange("p (h g) -> p h g", h=HEADS),
                                         bank[k][:, :].rearrange("p (h g) -> p h g", h=HEADS), over_slices, ALU.mult))
                then(v.tensor_tensor(bl_f[:, :].rearrange("p (h g) -> p h g", h=HEADS),
                                     bank[2][:, :].rearrange("p (h g) -> p h g", h=HEADS),
                                     bs[:, :].unsqueeze(1).to_broadcast([P, HEADS, SLICES]), ALU.add))
                then(v.tensor_tensor(bl_f[:, :].rearrange("p (h g) -> p h g", h=HEADS),
                                     bl_f[:, :].rearrange("p (h g) -> p h g", h=HEADS), over_slices, ALU.mult))
                v.wait_ge(big, 3 * 16)
                v.tensor_copy(W1H[:, :, :], w1[:, :, :])
                then(v.tensor_copy(CH[:, :, :], c_f[:, :, :]))
                v.tensor_tensor(W1L[:, :, :], w1[:, :, :], W1H[:, :, :].bitcast(F32), ALU.subtract)
                v.tensor_tensor(CL[:, :, :], c_f[:, :, :], CH[:, :, :].bitcast(F32), ALU.subtract)

                for b_f, b_rows, n in ((bz_f, bias_z, D), (bl_f, bias_l, HG), (bo_f, bias_o, D)):
                    then(v.tensor_copy(part[:, 0, 0:n], b_f[:, :]))
                    then(v.tensor_tensor(rest[:, 0, 0:n], b_f[:, :], part[:, 0, 0:n], ALU.subtract))
                    then(v.tensor_copy(part[:, 1, 0:n], rest[:, 0, 0:n]))
                    then(v.tensor_tensor(rest[:, 1, 0:n], rest[:, 0, 0:n], part[:, 1, 0:n], ALU.subtract))
                    then(v.tensor_copy(part[:, 2, 0:n], rest[:, 1, 0:n]))
                    then(v.tensor_scalar(acc[:, 0, 0:n], part[:, 0, 0:n], ident[:, 0:1], None, ALU.mult))
                    then(v.scalar_tensor_tensor(acc[:, 1, 0:n], part[:, 1, 0:n], ident[:, 1:2], acc[:, 0, 0:n],
                                                ALU.mult, ALU.add))
                    then(v.scalar_tensor_tensor(b_rows[:, :], part[:, 2, 0:n], ident[:, 2:3], acc[:, 1, 0:n],
                                                ALU.mult, ALU.add))
                for k in range(KC):
                    v.tensor_tensor(WfxA[:, k, :], WfxA[:, k, :], wfx_mid[:, :], ALU.subtract).then_inc(fx_sub, 1)

                v.wait_ge(again, 3 * 16)
                v.tensor_copy(rows_f[:, 0, :], dst_r[:, :])
                v.tensor_copy(rows_f[:, 1, :], src_r[:, :])
                v.tensor_copy(rows_f[:, 2, :], nxt_r[:, :]).then_inc(sorted_rows, 1)
                v.wait_ge(sorted_turned, 1)
                v.tensor_copy(key_col[:, :], bank[5][:, 0:CHUNKS])
                v.tensor_copy(src_i[:, :], bank[5][:, P:P + CHUNKS])
                then(v.tensor_copy(nxt_c[:, :], bank[5][:, 2 * P:2 * P + CHUNKS]))
                then(v.tensor_tensor(same[:, :], nxt_c[:, :], key_col[:, :], ALU.is_equal))
                then(v.scalar_tensor_tensor(tgt_f[:, :], same[:, :], float(SKIP), key_col[:, :], ALU.mult, ALU.add))
                then(v.tensor_copy(tgt_i[:, :], tgt_f[:, :]))

            @block.tensor
            def _(pe):
                pe.wait_ge(selected, 3)
                pe.wait_ge(raw_rows, 1)
                for i in range(2):
                    last = pe.transpose(bank[4][:, i * P:i * P + CHUNKS], rows_f[:, i, :], ident[0:CHUNKS, 0:CHUNKS])
                last.then_inc(raw_turned, 1)
                pe.wait_ge(down_ready, 1)
                pe.transpose(bank[7][0:1, 0:CHUNKS], down_c[:, :], ident[0:CHUNKS, 0:CHUNKS]).then_inc(down_turned, 1)
                pe.wait_ge(big, 3 * 16)
                for h in range(HEADS):
                    for k in range(KC):
                        last = pe.transpose(bank[h // 2][0:HD, (h % 2) * D + k * P:(h % 2) * D + (k + 1) * P],
                                            wx[:, k, h * HD:(h + 1) * HD], ident[:, :])
                    if h % 2:
                        last.then_inc(wx_turned, 1)
                pe.wait_ge(wx_copied, 4)
                pe.wait_ge(small, 14 * 16)
                for h in range(HEADS):
                    cols = slice(h * SLICES, (h + 1) * SLICES)
                    for k in range(KC):
                        pe.matmul(bank[k][:, cols], wxT[:, h, k * P:(k + 1) * P], ws[:, :], start=True, stop=True)
                    last = pe.matmul(bank[2][:, cols], bxT[:, h:h + 1].to_broadcast([HD, P]), ws[:, :],
                                     start=True, stop=True)
                last.then_inc(c_done, 1)
                pe.wait_ge(sorted_rows, 1)
                for i in range(3):
                    last = pe.transpose(bank[5][:, i * P:i * P + CHUNKS], rows_f[:, i, :], ident[0:CHUNKS, 0:CHUNKS])
                last.then_inc(sorted_turned, 1)

        with ExitStack() as stage:
            zeros = sb("zeros", [P, 7 * TILES * D], stack=stage)
            g_idx = sb("g_idx", [P, 4], I32, stack=stage)
            s_idx = sb("s_idx", [P, 4], I32, stack=stage)
            key = sb("key", [P, 8], stack=stage)
            xg = sb("xg", [P, 4, D], stack=stage)
            e_bn = sb("e_bn", [P, 4, 6], stack=stage)
            e_mv = sb("e_mv", [P, 4, 2], stack=stage)
            e_var = sb("e_var", [P, 4], stack=stage)
            e_rstd = sb("e_rstd", [P, 4], stack=stage)
            xe = sb("xe", [P, 4, D + 2], stack=stage)
            equal = sb("equal", [P, 2, P], stack=stage)
            carried = sb("carried", [P, 2, P], stack=stage)
            total = sb("total", [P, 4, D + 2], stack=stage)
            r_count = sb("r_count", [P, 2], stack=stage)
            mean = sb("mean", [P, 2, D], stack=stage)
            meanT = sb("meanT", [P, 2, D], stack=stage)
            product = sb("product", [P, 4, D], stack=stage)

            zero_set = sem("zeros_set")
            zeroed = sem("nbr_zeroed")
            ones_set = sem("edge_ones_set")
            indexed = sem("gather_index_ready")
            targeted = sem("scatter_index_ready")
            gathered = [sem(f"rows_gathered{i}") for i in range(4)]
            scattered_rows = [sem(f"rows_scattered{i}") for i in range(4)]
            e_stats = sem("edge_bn_stats")
            e_aggr = sem("edge_bn_aggr")
            e_eps = sem("edge_var_eps")
            e_pow = sem("edge_rstd")
            xe_ready = sem("xe_ready")
            spread = sem("keys_spread")
            masks = sem("masks_ready")
            summed = sem("sums_done")
            total_ready = sem("totals_ready")
            count_ready = sem("r_count_ready")
            mean_ready = sem("means_ready")
            mean_turned = sem("means_turned")
            meanT_ready = sem("meanT_ready")
            multiplied = sem("products_done")
            product_ready = sem("products_ready")

            U = 8
            block = stage.enter_context(nc.Block())

            @block.sync
            def _(sp):
                sp.wait_ge(zero_set, 1)
                assert GROUPS % 7 == 0
                for q in range(GROUPS // 7):
                    sp.dma_start(nbr_g[7 * q:7 * q + 7].rearrange("g p d -> p g d"),
                                 zeros[:, :].rearrange("p (g d) -> p g d", g=7)).then_inc(zeroed, 16)
                sp.wait_ge(zeroed, 16 * (GROUPS // 7))
                for i in range(4):
                    sp.wait_ge(scattered_rows[i], 16 * len(range(i, CHUNKS, 4)))

            @block.gpsimd
            def _(pool):
                pool.memset(xe[:, :, D:D + 1], 1.0).then_inc(ones_set, 1)
                pool.memset(xe[:, :, D + 1:D + 2], 0.0).then_inc(ones_set, 1)

                def step(turn, j):
                    n = turn * U + j
                    if inside(n, CHUNKS):
                        at_least(pool, xe_ready, n - 3)
                        pool.wait_ge(indexed, n + 1)
                        gate(pool)
                        pool.indirect_dma_start(xg[:, j % 4, :], None, x,
                                                bass.IndirectOffsetOnAxis(ap=g_idx[:, j % 4:j % 4 + 1], axis=0)
                                                ).then_inc(gathered[j % 4], 16)
                    n = turn * U + j - 2
                    if inside(n, CHUNKS):
                        r = (j - 2) % 4
                        pool.wait_ge(e_eps, n + 1)
                        pool.tensor_tensor(e_rstd[:, r:r + 1], e_var[:, r:r + 1], minus_half[:, 0:1],
                                           ALU.pow).then_inc(e_pow, 1)
                    n = turn * U + j - 8
                    if inside(n, CHUNKS):
                        r = j % 4
                        pool.wait_ge(zeroed, 16 * (GROUPS // 7))
                        pool.wait_ge(targeted, n + 1)
                        pool.wait_ge(product_ready, n + 1)
                        gate(pool)
                        pool.indirect_dma_start(nbr, bass.IndirectOffsetOnAxis(ap=s_idx[:, r:r + 1], axis=0),
                                                product[:, r, :], None, bounds_check=NODES - 1,
                                                oob_is_err=False).then_inc(scattered_rows[r], 16)

                run_steps(pool, CHUNKS, 8, U, 1, step)

            @block.vector
            def _(v):
                v.memset(zeros[:, :], 0.0).then_inc(zero_set, 1)

                def step(turn, j):
                    n = turn * U + j
                    if inside(n, CHUNKS):
                        r = j % 4
                        at_least(v, gathered[r], (turn * 2 + j // 4) * 16)
                        gate(v)
                        v.tensor_copy(key[:, j:j + 1], key_col[:, bass.ds(n, 1)])
                        v.tensor_copy(g_idx[:, r:r + 1], src_i[:, bass.ds(n, 1)]).then_inc(indexed, 1)
                    n = turn * U + j - 2
                    if inside(n, CHUNKS):
                        r = (j - 2) % 4
                        v.wait_ge(gathered[r], (turn * 2 + (j - 2) // 4) * 16 + 16)
                        v.bn_stats(e_bn[:, r, :], xg[:, r, :]).then_inc(e_stats, 1)
                        v.wait_ge(e_stats, n + 1)
                        gate(v)
                        v.bn_aggr(e_mv[:, r, :], e_bn[:, r, :]).then_inc(e_aggr, 1)
                        v.wait_ge(e_aggr, n + 1)
                        v.tensor_scalar(e_var[:, r:r + 1], e_mv[:, r, 1:2], LN_EPS, None, ALU.add).then_inc(e_eps, 1)
                    n = turn * U + j - 3
                    if inside(n, CHUNKS):
                        r, m = (j - 3) % 4, (j - 3) % 2
                        v.wait_ge(spread, n + 1)
                        at_least(v, summed, n - 1)
                        if not (isinstance(n, int) and n == 0):
                            v.tensor_scalar(carried[:, m, :], bank[m][:, 0:P], key[:, (j - 4) % 8:(j - 4) % 8 + 1],
                                            last_row[:, 0:1], ALU.is_equal, ALU.mult)
                        v.tensor_scalar(equal[:, m, :], bank[m][:, 0:P], key[:, (j - 3) % 8:(j - 3) % 8 + 1], None,
                                        ALU.is_equal).then_inc(masks, 1)
                        v.wait_ge(e_pow, n + 1)
                        v.tensor_scalar(xe[:, r, 0:D], xg[:, r, :], e_mv[:, r, 0:1], e_rstd[:, r:r + 1],
                                        ALU.subtract, ALU.mult).then_inc(xe_ready, 1)
                    n = turn * U + j - 5
                    if inside(n, CHUNKS):
                        r, m = (j - 5) % 4, (j - 5) % 2
                        v.wait_ge(total_ready, n + 1)
                        v.reciprocal(r_count[:, m:m + 1], total[:, r, D:D + 1]).then_inc(count_ready, 1)
                        at_least(v, mean_turned, n - 1)
                        v.wait_ge(count_ready, n + 1)
                        v.tensor_scalar(mean[:, m, :], total[:, r, 0:D], r_count[:, m:m + 1], None,
                                        ALU.mult).then_inc(mean_ready, 1)
                    n = turn * U + j - 7
                    if inside(n, CHUNKS):
                        r = (j - 7) % 4
                        at_least(v, scattered_rows[r], (turn * 2 + (j - 7) // 4) * 16)
                        gate(v)
                        v.tensor_copy(s_idx[:, r:r + 1], tgt_i[:, bass.ds(n, 1)]).then_inc(targeted, 1)

                run_steps(v, CHUNKS, 8, U, 1, step)

            @block.tensor
            def _(pe):
                pe.wait_ge(ones_set, 2)

                def step(turn, j):
                    n = turn * U + j - 2
                    if inside(n, CHUNKS):
                        pe.wait_ge(indexed, n + 1)
                        at_least(pe, masks, n - 1)
                        r = (j - 2) % 8
                        pe.matmul(bank[(j - 2) % 2][:, 0:P], key[:, r:r + 1].to_broadcast([P, P]), ident[:, :],
                                  start=True, stop=True).then_inc(spread, 1)
                    n = turn * U + j - 4
                    if inside(n, CHUNKS):
                        r, m = (j - 4) % 4, (j - 4) % 2
                        first = isinstance(n, int) and n == 0
                        pe.wait_ge(masks, n + 1)
                        pe.wait_ge(xe_ready, n + 1)
                        last = pe.matmul(bank[2 + m][:, 0:D + 2], equal[:, m, :], xe[:, r, :], start=True, stop=first)
                        if not first:
                            pe.wait_ge(total_ready, n)
                            last = pe.matmul(bank[2 + m][:, 0:D + 2], carried[:, m, :], total[:, (j - 5) % 4, :],
                                             start=False, stop=True)
                        last.then_inc(summed, 1)
                    n = turn * U + j - 6
                    if inside(n, CHUNKS):
                        m = (j - 6) % 2
                        pe.wait_ge(mean_ready, n + 1)
                        at_least(pe, meanT_ready, n - 1)
                        for k in range(KC):
                            last = pe.transpose(bank[4 + m][:, k * P:(k + 1) * P], mean[:, m, k * P:(k + 1) * P],
                                                ident[:, :])
                        last.then_inc(mean_turned, 1)
                    n = turn * U + j - 7
                    if inside(n, CHUNKS):
                        m = (j - 7) % 2
                        pe.wait_ge(meanT_ready, n + 1)
                        at_least(pe, product_ready, n - 1)
                        for k in range(KC):
                            last = pe.matmul(bank[6 + m][:, 0:D], meanT[:, m, k * P:(k + 1) * P], W2[:, k, :],
                                             start=(k == 0), stop=(k == KC - 1))
                        last.then_inc(multiplied, 1)

                run_steps(pe, CHUNKS, 8, U, 1, step)

            @block.scalar
            def _(act):
                def step(turn, j):
                    n = turn * U + j - 4
                    if inside(n, CHUNKS):
                        r, m = (j - 4) % 4, (j - 4) % 2
                        at_least(act, mean_ready, n - 3)
                        act.wait_ge(summed, n + 1)
                        act.activation(total[:, r, :], bank[2 + m][:, 0:D + 2], ACT.Copy).then_inc(total_ready, 1)
                    n = turn * U + j - 6
                    if inside(n, CHUNKS):
                        m = (j - 6) % 2
                        at_least(act, multiplied, n - 1)
                        act.wait_ge(mean_turned, n + 1)
                        act.activation(meanT[:, m, :], bank[4 + m][:, 0:D], ACT.Copy).then_inc(meanT_ready, 1)
                    n = turn * U + j - 7
                    if inside(n, CHUNKS):
                        r, m = (j - 7) % 4, (j - 7) % 2
                        at_least(act, scattered_rows[r], (turn * 2 + (j - 7) // 4) * 16)
                        act.wait_ge(multiplied, n + 1)
                        act.activation(product[:, r, :], bank[6 + m][:, 0:D], ACT.Copy).then_inc(product_ready, 1)

                run_steps(act, CHUNKS, 8, U, 1, step)

        with ExitStack() as stage:
            xs = sb("xs", [P, 4, TILES, D], stack=stage)
            ns = sb("ns", [P, 4, TILES, D], stack=stage)
            bn1 = sb("bn1", [P, 2, 2, 6], stack=stage)
            mv1 = sb("mv1", [P, 2, 2, 2], stack=stage)
            var1 = sb("var1", [P, 2, 2], stack=stage)
            rstd1 = sb("rstd1", [P, 2, 2], stack=stage)
            xn = sb("xn", [P, 2, 2 * D], stack=stage)
            xnH = sb("xnH", [P, 2, 2 * D], F32R, stack=stage)
            xnL = sb("xnL", [P, 2, 2 * D], F32R, stack=stage)
            xnTH = sb("xnTH", [P, 2, 2 * D], F32R, stack=stage)
            xnTL = sb("xnTL", [P, 2, 2 * D], F32R, stack=stage)
            z = sb("z", [P, 2, 2 * D], stack=stage)
            relu = sb("relu", [P, 4, 2 * D], stack=stage)
            square = sb("square", [P, 2 * D], stack=stage)
            norm2 = sb("norm2", [P, 2, 2], stack=stage)
            norm2c = sb("norm2c", [P, 2, 2], stack=stage)
            inv = sb("inv", [P, 2, 2], stack=stage)
            x1 = sb("x1", [P, 4, TILES, D], stack=stage)
            bn2 = sb("bn2", [P, 2, 2, 6], stack=stage)
            mv2 = sb("mv2", [P, 2, 2, 2], stack=stage)
            var2 = sb("var2", [P, 2, 2], stack=stage)
            rstd2 = sb("rstd2", [P, 2, 2], stack=stage)
            y = sb("y", [P, 2, 2, D], stack=stage)
            yH = sb("yH", [P, 8, 2, D + 1], F32R, stack=stage)
            yL = sb("yL", [P, 8, 2, D + 1], F32R, stack=stage)
            yTH = sb("yTH", [P, 2, 2 * D], F32R, stack=stage)
            yTL = sb("yTL", [P, 2, 2 * D], F32R, stack=stage)
            top = sb("top", [P, 2, 2 * HEADS], stack=stage)
            e = sb("e", [P, 2, 2 * HG], stack=stage)
            esum = sb("esum", [P, 2, 2 * HEADS], stack=stage)
            erec = sb("erec", [P, 2, 2 * HEADS], stack=stage)
            w = sb("w", [P, 2, 2 * HG], stack=stage)
            wH = sb("wH", [P, 2, 2 * HG], F32R, stack=stage)
            wL = sb("wL", [P, 2, 2 * HG], F32R, stack=stage)
            wT = sb("wT", [P, 4, 2 * HG], stack=stage)
            zero_bf = sb("zero_bf", [P, P], BF16, stack=stage)

            x_in = [sem(f"x_in{i}") for i in range(4)]
            x1_out = [sem(f"x1_out{i}") for i in range(4)]
            wT_out = [sem(f"wT_out{i}") for i in range(4)]
            ones_y = sem("y_ones_set")
            stats1 = sem("stats1")
            aggr1 = sem("aggr1")
            var1_ready = sem("var1_ready")
            rstd1_ready = sem("rstd1_ready")
            xn_ready = sem("xn_ready")
            xnH_ready = sem("xnH_ready")
            xnL_ready = sem("xnL_ready")
            xn_turned = sem("xn_turned")
            xnT_ready = sem("xnT_ready")
            z_done = sem("z_done")
            z_ready = sem("z_ready")
            relu_ready = sem("relu_ready")
            norm2_ready = sem("norm2_ready")
            norm2c_ready = sem("norm2c_ready")
            inv_ready = sem("inv_ready")
            x1_ready = sem("x1_ready")
            stats2 = sem("stats2")
            aggr2 = sem("aggr2")
            var2_ready = sem("var2_ready")
            rstd2_ready = sem("rstd2_ready")
            y_ready = sem("y_ready")
            yH_ready = sem("yH_ready")
            yL_ready = sem("yL_ready")
            y_turned = sem("y_turned")
            yT_ready = sem("yT_ready")
            logits_done = sem("logits_done")
            top_ready = sem("top_ready")
            shifted = sem("logits_shifted")
            exp_ready = sem("exp_ready")
            esum_ready = sem("esum_ready")
            erec_ready = sem("erec_ready")
            w_ready = sem("w_ready")
            wH_ready = sem("wH_ready")
            wL_ready = sem("wL_ready")
            w_turned = sem("w_turned")
            wT_ready = sem("wT_ready")
            sums_in = sem("token_sums_in")

            BTH, BTL, BZ, BL, BW, BS = 0, 1, 2, 3, 5, 6
            U = 8
            LAG = 8
            block = stage.enter_context(nc.Block())

            def heads(ap):
                return ap.rearrange("p (h g) -> p h g", g=SLICES)

            def flat(ap):
                return ap.rearrange("p t d -> p (t d)")

            @block.sync
            def _(sp):
                def step(turn, j):
                    g = turn * U + j
                    if inside(g, GROUPS):
                        r = j % 4
                        at_least(sp, x1_ready, 2 * g - 6)
                        if isinstance(g, int) and g == GROUPS - 1:
                            sp.dma_start(flat(xs[0:LAST_ROWS, r]), x_last).then_inc(x_in[r], 16)
                        else:
                            sp.dma_start(flat(xs[:, r]), row(x_g, g)).then_inc(x_in[r], 16)
                        sp.dma_start(flat(ns[:, r]), row(nbr_g, g)).then_inc(x_in[r], 16)
                    g = turn * U + j - 3
                    if inside(g, GROUPS):
                        r = (j - 3) % 4
                        sp.wait_ge(x1_ready, 2 * g + 2)
                        sp.dma_start(row(x1_g, g), flat(x1[:, r])).then_inc(x1_out[r], 16)
                    for t in range(2):
                        n = (turn * U + j - 5) * 2 + t
                        if inside(n, PAIRS):
                            r = ((j - 5) * 2 + t) % 4
                            sp.wait_ge(wT_ready, 2 * n + 2)
                            sp.dma_start(row(wT_s, n), wT[:, r, :]).then_inc(wT_out[r], 16)

                run_steps(sp, GROUPS, 5, U, 1, step)
                for i in range(4):
                    sp.wait_ge(x1_out[i], 16 * len(range(i, GROUPS, 4)))
                    sp.wait_ge(wT_out[i], 16 * len(range(i, PAIRS, 4)))

            @block.gpsimd
            def _(pool):
                pool.memset(yH[:, :, :, D:D + 1].bitcast(F32), 1.0).then_inc(ones_y, 1)
                pool.memset(yL[:, :, :, D:D + 1].bitcast(F32), 0.0).then_inc(ones_y, 1)
                pool.memset(zero_bf[:, :], 0.0).then_inc(ones_y, 1)

                def step(turn, j):
                    n = turn * U + j - 4
                    if inside(n, PAIRS):
                        r = (j - 4) % 2
                        at_least(pool, x1_ready, n - 1)
                        pool.wait_ge(norm2c_ready, n + 1)
                        pool.tensor_tensor(inv[:, r, :], norm2c[:, r, :], minus_half[:, 0:2],
                                           ALU.pow).then_inc(inv_ready, 1)
                    n = turn * U + j - 5
                    if inside(n, PAIRS):
                        pool.wait_ge(yH_ready, n + 1)
                        pool.tensor_tensor(yL[:, (j - 5) % 8, :, 0:D], y[:, (j - 5) % 2, :, :],
                                           yH[:, (j - 5) % 8, :, 0:D].bitcast(F32), ALU.subtract).then_inc(yL_ready, 1)
                    n = turn * U + j
                    if inside(n, PAIRS):
                        r = j % 2
                        at_least(pool, xn_ready, n - 1)
                        pool.wait_ge(var1_ready, n + 1)
                        pool.tensor_tensor(rstd1[:, r, :], var1[:, r, :], minus_half[:, 0:2],
                                           ALU.pow).then_inc(rstd1_ready, 1)
                    n = turn * U + j - 7
                    if inside(n, PAIRS):
                        r = (j - 7) % 2
                        at_least(pool, wL_ready, n - 1)
                        pool.wait_ge(erec_ready, n + 1)
                        pool.tensor_tensor(heads(w[:, r, :]), heads(e[:, r, :]),
                                           erec[:, r, :].unsqueeze(2).to_broadcast([P, 2 * HEADS, SLICES]),
                                           ALU.mult).then_inc(w_ready, 1)
                    n = turn * U + j - 1
                    if inside(n, PAIRS):
                        r = (j - 1) % 2
                        at_least(pool, xn_turned, n - 1)
                        pool.wait_ge(xnH_ready, n + 1)
                        pool.tensor_tensor(xnL[:, r, :], xn[:, r, :], xnH[:, r, :].bitcast(F32),
                                           ALU.subtract).then_inc(xnL_ready, 1)
                    n = turn * U + j - 4
                    if inside(n, PAIRS):
                        r = (j - 4) % 2
                        at_least(pool, y_ready, n - 1)
                        pool.wait_ge(var2_ready, n + 1)
                        pool.tensor_tensor(rstd2[:, r, :], var2[:, r, :], minus_half[:, 0:2],
                                           ALU.pow).then_inc(rstd2_ready, 1)
                    n = turn * U + j - 7
                    if inside(n, PAIRS):
                        r = (j - 7) % 2
                        at_least(pool, sums_in, n - 1)
                        pool.wait_ge(wH_ready, n + 1)
                        pool.tensor_tensor(wL[:, r, :], w[:, r, :], wH[:, r, :].bitcast(F32),
                                           ALU.subtract).then_inc(wL_ready, 1)

                run_steps(pool, PAIRS, LAG, U, 2, step)

            @block.vector
            def _(v):
                def step(turn, j):
                    n = turn * U + j - 4
                    if inside(n, PAIRS):
                        r = (j - 4) % 2
                        v.wait_ge(norm2_ready, n + 1)
                        v.tensor_scalar(norm2c[:, r, :], norm2[:, r, :], NORM_EPS * NORM_EPS, None,
                                        ALU.max).then_inc(norm2c_ready, 1)
                    n = turn * U + j - 5
                    if inside(n, PAIRS):
                        r, gslot, t0 = (j - 5) % 2, ((j - 5) // 2) % 4, ((j - 5) % 2) * 2
                        at_least(v, yL_ready, n - 1)
                        v.wait_ge(rstd2_ready, n + 1)
                        gate(v)
                        for t in range(2):
                            last = v.tensor_scalar(y[:, r, t, :], x1[:, gslot, t0 + t, :],
                                                   mv2[:, r, t, 0:1], rstd2[:, r, t:t + 1],
                                                   ALU.subtract, ALU.mult)
                        last.then_inc(y_ready, 1)
                    n = turn * U + j - 3
                    if inside(n, PAIRS):
                        r, gslot, t0 = (j - 3) % 2, ((j - 3) // 2) % 4, ((j - 3) % 2) * 2
                        at_least(v, relu_ready, n - 1)
                        v.wait_ge(z_done, n + 1)
                        v.tensor_tensor(z[:, r, :], bank[BZ][:, :], flat(ns[:, gslot, t0:t0 + 2, :]),
                                        ALU.add).then_inc(z_ready, 1)
                    n = turn * U + j
                    if inside(n, PAIRS):
                        r, gslot, t0 = j % 2, (j // 2) % 4, (j % 2) * 2
                        v.wait_ge(x_in[gslot], turn * 32 + 32)
                        for t in range(2):
                            last = v.bn_stats(bn1[:, r, t, :], xs[:, gslot, t0 + t, :])
                        last.then_inc(stats1, 1)
                        v.wait_ge(stats1, n + 1)
                        gate(v)
                        for t in range(2):
                            last = v.bn_aggr(mv1[:, r, t, :], bn1[:, r, t, :])
                        last.then_inc(aggr1, 1)
                        v.wait_ge(aggr1, n + 1)
                        v.tensor_scalar(var1[:, r, :], mv1[:, r, :, 1], LN_EPS, None, ALU.add).then_inc(var1_ready, 1)
                    n = turn * U + j - 7
                    if inside(n, PAIRS):
                        r = (j - 7) % 2
                        v.wait_ge(exp_ready, n + 1)
                        v.reduce_sum(esum[:, r, :], heads(e[:, r, :]), AX).then_inc(esum_ready, 1)
                        at_least(v, w_ready, n - 1)
                        v.wait_ge(esum_ready, n + 1)
                        v.reciprocal(erec[:, r, :], esum[:, r, :]).then_inc(erec_ready, 1)
                    n = turn * U + j - 1
                    if inside(n, PAIRS):
                        r, gslot, t0 = (j - 1) % 2, ((j - 1) // 2) % 4, ((j - 1) % 2) * 2
                        at_least(v, xnL_ready, n - 1)
                        v.wait_ge(rstd1_ready, n + 1)
                        gate(v)
                        for t in range(2):
                            last = v.tensor_scalar(xn[:, r, t * D:(t + 1) * D], xs[:, gslot, t0 + t, :],
                                                   mv1[:, r, t, 0:1], rstd1[:, r, t:t + 1], ALU.subtract, ALU.mult)
                        last.then_inc(xn_ready, 1)
                    n = turn * U + j - 4
                    if inside(n, PAIRS):
                        r, gslot, t0 = (j - 4) % 2, ((j - 4) // 2) % 4, ((j - 4) % 2) * 2
                        v.wait_ge(inv_ready, n + 1)
                        if (j - 4) % 2 == 0:
                            at_least(v, x1_out[gslot], (turn + (j - 4) // 8) * 16)
                        for t in range(2):
                            last = v.scalar_tensor_tensor(x1[:, gslot, t0 + t, :],
                                                          relu[:, (j - 4) % 4, t * D:(t + 1) * D],
                                                          inv[:, r, t:t + 1], xs[:, gslot, t0 + t, :],
                                                          ALU.mult, ALU.add)
                        last.then_inc(x1_ready, 1)
                        v.wait_ge(x1_ready, n + 1)
                        for t in range(2):
                            last = v.bn_stats(bn2[:, r, t, :], x1[:, gslot, t0 + t, :])
                        last.then_inc(stats2, 1)
                        v.wait_ge(stats2, n + 1)
                        gate(v)
                        for t in range(2):
                            last = v.bn_aggr(mv2[:, r, t, :], bn2[:, r, t, :])
                        last.then_inc(aggr2, 1)
                        v.wait_ge(aggr2, n + 1)
                        v.tensor_scalar(var2[:, r, :], mv2[:, r, :, 1], LN_EPS, None, ALU.add).then_inc(var2_ready, 1)
                    n = turn * U + j - 6
                    if inside(n, PAIRS):
                        r = (j - 6) % 2
                        at_least(v, w_ready, n - 1)
                        for t in range(2):
                            v.wait_ge(logits_done, 2 * n + t + 1)
                            v.reduce_max(top[:, r, t * HEADS:(t + 1) * HEADS], heads(bank[BL + t][:, :]),
                                         AX).then_inc(top_ready, 1)
                            v.wait_ge(top_ready, 2 * n + t + 1)
                            v.tensor_tensor(heads(e[:, r, t * HG:(t + 1) * HG]), heads(bank[BL + t][:, :]),
                                            top[:, r, t * HEADS:(t + 1) * HEADS].unsqueeze(2).to_broadcast([P, HEADS, SLICES]),
                                            ALU.subtract).then_inc(shifted, 1)

                run_steps(v, PAIRS, LAG, U, 2, step)

            @block.scalar
            def _(act):
                def step(turn, j):
                    def w_out(t):
                        n = turn * U + j - 8
                        if inside(n, PAIRS):
                            r = j % 4
                            if t == 0:
                                at_least(act, wT_out[r], (turn * 2 + (j - 8) // 4) * 16)
                            act.wait_ge(w_turned, 2 * n + t + 1)
                            act.activation(wT[:, r, t * HG:(t + 1) * HG], bank[BW][:, :], ACT.Copy).then_inc(wT_ready, 1)

                    n = turn * U + j - 2
                    if inside(n, PAIRS):
                        r = (j - 2) % 2
                        at_least(act, z_done, n - 1)
                        act.wait_ge(xn_turned, n + 1)
                        act.activation(xnTH[:, r, :], bank[BTH][:, :], ACT.Copy)
                        act.activation(xnTL[:, r, :], bank[BTL][:, :], ACT.Copy).then_inc(xnT_ready, 1)
                    n = turn * U + j - 5
                    if inside(n, PAIRS):
                        at_least(act, sums_in, n - 7)
                        act.wait_ge(y_ready, n + 1)
                        act.activation(yH[:, (j - 5) % 8, :, 0:D], y[:, (j - 5) % 2, :, :], ACT.Copy).then_inc(yH_ready, 1)
                    n = turn * U + j - 3
                    if inside(n, PAIRS):
                        r, q = (j - 3) % 2, (j - 3) % 4
                        at_least(act, x1_ready, n - 3)
                        act.wait_ge(z_ready, n + 1)
                        act.activation(relu[:, q, :], z[:, r, :], ACT.Relu).then_inc(relu_ready, 1)
                        at_least(act, norm2c_ready, n - 1)
                        act.wait_ge(relu_ready, n + 1)
                        at_least(act, norm2_ready, n)
                        for t in range(2):
                            last = act.activation(square[:, t * D:(t + 1) * D], relu[:, q, t * D:(t + 1) * D],
                                                  ACT.Square, accum_out=norm2[:, r, t:t + 1])
                        last.then_inc(norm2_ready, 1)
                    n = turn * U + j - 1
                    if inside(n, PAIRS):
                        r = (j - 1) % 2
                        at_least(act, xn_turned, n - 1)
                        act.wait_ge(xn_ready, n + 1)
                        act.activation(xnH[:, r, :], xn[:, r, :], ACT.Copy).then_inc(xnH_ready, 1)
                    n = turn * U + j - 5
                    if inside(n, PAIRS):
                        r = (j - 5) % 2
                        at_least(act, logits_done, 2 * n - 2)
                        act.wait_ge(y_turned, n + 1)
                        act.activation(yTH[:, r, :], bank[BTH][:, :], ACT.Copy)
                        act.activation(yTL[:, r, :], bank[BTL][:, :], ACT.Copy).then_inc(yT_ready, 1)
                    w_out(0)
                    n = turn * U + j - 7
                    if inside(n, PAIRS):
                        r = (j - 7) % 2
                        at_least(act, sums_in, n - 1)
                        act.wait_ge(w_ready, n + 1)
                        act.activation(wH[:, r, :], w[:, r, :], ACT.Copy).then_inc(wH_ready, 1)
                    w_out(1)
                    n = turn * U + j - 6
                    if inside(n, PAIRS):
                        r = (j - 6) % 2
                        act.wait_ge(shifted, 2 * n + 2)
                        act.activation(e[:, r, :], e[:, r, :], ACT.Exp).then_inc(exp_ready, 1)

                run_steps(act, PAIRS, LAG, U, 2, step)

            @block.tensor
            def _(pe):
                pe.wait_ge(ones_y, 3)
                for k in range(KC):
                    pe.matmul(bank[BS + k][:, :], zero_bf[:, :], bias_l[:, :], start=True, stop=False)

                def turn_parts(high, low):
                    for to, part in ((bank[BTH], high), (bank[BTL], low)):
                        for t in range(2):
                            for k in range(KC):
                                last = pe.transpose(to[:, t * D + k * P:t * D + (k + 1) * P].bitcast(F32R),
                                                    part(t, k), ident_r[:, :])
                    return last

                def step(turn, j):
                    n = turn * U + j - 2
                    if inside(n, PAIRS):
                        r = (j - 2) % 2
                        pe.wait_ge(xnL_ready, n + 1)
                        at_least(pe, yT_ready, n - 3)
                        turn_parts(lambda t, k: xnH[:, r, t * D + k * P:t * D + (k + 1) * P],
                                   lambda t, k: xnL[:, r, t * D + k * P:t * D + (k + 1) * P]).then_inc(xn_turned, 1)
                    n = turn * U + j - 6
                    if inside(n, PAIRS):
                        r = (j - 6) % 2
                        pe.wait_ge(yT_ready, n + 1)
                        for t in range(2):
                            at_least(pe, shifted, 2 * n + t - 1)
                            pe.matmul(bank[BL + t][:, :], ones_bf[:, :], bias_l[:, :], start=True, stop=False)
                            for k in range(KC):
                                at = slice(t * D + k * P, t * D + (k + 1) * P)
                                pe.matmul(bank[BL + t][:, :], yTH[:, r, at], CL[:, k, :], start=False, stop=False)
                                pe.matmul(bank[BL + t][:, :], yTL[:, r, at], CH[:, k, :], start=False, stop=False)
                                last = pe.matmul(bank[BL + t][:, :], yTH[:, r, at], CH[:, k, :], start=False,
                                                 stop=(k == KC - 1))
                            last.then_inc(logits_done, 1)
                    n = turn * U + j - 2
                    if inside(n, PAIRS):
                        r = (j - 2) % 2
                        pe.wait_ge(xnT_ready, n + 1)
                        at_least(pe, z_ready, n)
                        for t in range(2):
                            to = bank[BZ][:, t * D:(t + 1) * D]
                            pe.matmul(to, ones_bf[:, :], bias_z[:, :], start=True, stop=False)
                            for k in range(KC):
                                at = slice(t * D + k * P, t * D + (k + 1) * P)
                                pe.matmul(to, xnTH[:, r, at], W1L[:, k, :], start=False, stop=False)
                                pe.matmul(to, xnTL[:, r, at], W1H[:, k, :], start=False, stop=False)
                                last = pe.matmul(to, xnTH[:, r, at], W1H[:, k, :], start=False, stop=(k == KC - 1))
                        last.then_inc(z_done, 1)
                    n = turn * U + j - 5
                    if inside(n, PAIRS):
                        r = (j - 5) % 8
                        pe.wait_ge(yL_ready, n + 1)
                        at_least(pe, xnT_ready, n + 4 if not isinstance(n, int) else min(n + 4, PAIRS))
                        turn_parts(lambda t, k: yH[:, r, t, k * P:(k + 1) * P],
                                   lambda t, k: yL[:, r, t, k * P:(k + 1) * P]).then_inc(y_turned, 1)
                    n = turn * U + j - 8
                    if inside(n, PAIRS):
                        r, ry = (j - 8) % 2, (j - 8) % 8
                        rows = LAST_ROWS if isinstance(n, int) and n >= PAIRS - 2 else P
                        pe.wait_ge(wL_ready, n + 1)
                        for t in range(2):
                            at_least(pe, wT_ready, 2 * n + t)
                            for k in range(HC):
                                to, at = bank[BW][:, k * P:(k + 1) * P], slice(t * HG + k * P, t * HG + (k + 1) * P)
                                pe.matmul(to, wH[:, r, at], ident_r[:, :], start=True, stop=False)
                                last = pe.matmul(to, wL[:, r, at], ident_r[:, :], start=False, stop=True)
                            last.then_inc(w_turned, 1)
                            all_w = slice(t * HG, (t + 1) * HG)
                            for k in range(KC):
                                at = slice(k * (P + 1), k * (P + 1) + P)
                                end = isinstance(n, int) and n == PAIRS - 1 and t == 1
                                pe.matmul(bank[BS + k][:, :], yH[0:rows, ry, t, at], wL[0:rows, r, all_w],
                                          start=False, stop=False)
                                pe.matmul(bank[BS + k][:, :], yL[0:rows, ry, t, at], wH[0:rows, r, all_w],
                                          start=False, stop=False)
                                last = pe.matmul(bank[BS + k][:, :], yH[0:rows, ry, t, at], wH[0:rows, r, all_w],
                                                 start=False, stop=end)
                        last.then_inc(sums_in, 1)

                run_steps(pe, PAIRS, LAG, U, 2, step)

        MH = sb("MH", [P, HC, D], F32R)
        ML = sb("ML", [P, HC, D], F32R)
        with ExitStack() as stage:
            zt = sb("zt", [P, KC, HG], stack=stage)
            norm_b = sb("norm_b", [P, HG], stack=stage)
            norm_r = sb("norm_r", [P, HG], stack=stage)
            ztn = sb("ztn", [P, KC, HG], stack=stage)
            tokT = sb("tokT", [HD, HG], stack=stage)
            qT = sb("qT", [HD, HG], stack=stage)
            kT = sb("kT", [HD, HG], stack=stage)
            val = sb("val", [HD, HG], stack=stage)
            amax = sb("amax", [HD, HEADS], stack=stage)
            att = sb("att", [HD, HG], stack=stage)
            asum = sb("asum", [HD, HEADS], stack=stage)
            arec = sb("arec", [HD, HEADS], stack=stage)
            attn = sb("attn", [HD, HG], stack=stage)
            attT = sb("attT", [HD, HG], stack=stage)
            oT = sb("oT", [HD, HG], stack=stage)
            m_head = sb("m_head", [SLICES, HEADS, D], stack=stage)
            M = sb("M", [P, HC, D], stack=stage)

            tv = sem("tokens_vector")
            tp = sem("tokens_tensor")
            ta = sem("tokens_scalar")
            m_in = sem("m_in")
            block = stage.enter_context(nc.Block())

            def hs(h):
                return slice(h * HD, (h + 1) * HD)

            def by_head(ap):
                return ap.rearrange("p (h g) -> p h g", h=HEADS)

            @block.tensor
            def _(pe):
                pe.wait_ge(tv, 1)
                pe.matmul(bank[0][:, :], pick_last[:, :], zt[:, 1, :], start=True, stop=True).then_inc(tp, 1)
                pe.wait_ge(tv, 5)
                for h in range(HEADS):
                    for k in range(KC):
                        last = pe.matmul(bank[1][0:HD, hs(h)], WfxA[:, k, hs(h)], ztn[:, k, hs(h)],
                                         start=(k == 0), stop=(k == KC - 1))
                last.then_inc(tp, 1)
                pe.wait_ge(tv, 6)
                pe.matmul(bank[2][0:HD, :], wq[:, :], tokT[:, :], start=True, stop=True)
                pe.matmul(bank[3][0:HD, :], wk[:, :], tokT[:, :], start=True, stop=True)
                for h in range(HEADS):
                    last = pe.matmul(bank[4][0:HD, hs(h)], tokT[:, hs(h)], wv[:, :], start=True, stop=True)
                last.then_inc(tp, 1)
                pe.wait_ge(tv, 9)
                for h in range(HEADS):
                    last = pe.matmul(bank[5][0:HD, hs(h)], qT[:, hs(h)], kT[:, hs(h)], start=True, stop=True)
                last.then_inc(tp, 1)
                pe.wait_ge(tv, 14)
                for h in range(HEADS):
                    last = pe.transpose(bank[0][0:HD, hs(h)], attn[:, hs(h)], ident[0:HD, 0:HD])
                last.then_inc(tp, 1)
                pe.wait_ge(tv, 15)
                for h in range(HEADS):
                    last = pe.matmul(bank[1][0:HD, hs(h)], val[:, hs(h)], attT[:, hs(h)], start=True, stop=True)
                last.then_inc(tp, 1)
                pe.wait_ge(tv, 16)
                for h in range(HEADS):
                    last = pe.matmul(bank[2 + h // 2][0:SLICES, (h % 2) * D:(h % 2 + 1) * D], oT[:, hs(h)],
                                     wo[:, h, :], start=True, stop=True)
                last.then_inc(tp, 1)

            @block.vector
            def _(v):
                done = [0]

                def then(instruction):
                    instruction.then_inc(tv, 1)
                    done[0] += 1
                    v.wait_ge(tv, done[0])

                v.tensor_copy(zt[:, 0, :], bank[6][:, :])
                then(v.tensor_copy(zt[:, 1, :], bank[7][:, :]))
                v.wait_ge(tp, 1)
                then(v.tensor_scalar(norm_b[:, :], bank[0][:, :], 1e-5, None, ALU.add))
                then(v.reciprocal(norm_r[:, :], norm_b[:, :]))
                for k in range(KC):
                    then(v.tensor_tensor(ztn[:, k, :], zt[:, k, :], norm_r[:, :], ALU.mult))
                v.wait_ge(tp, 2)
                then(v.tensor_copy(tokT[:, :], bank[1][0:HD, :]))
                v.wait_ge(tp, 3)
                then(v.tensor_copy(qT[:, :], bank[2][0:HD, :]))
                then(v.tensor_copy(kT[:, :], bank[3][0:HD, :]))
                then(v.tensor_copy(val[:, :], bank[4][0:HD, :]))
                v.wait_ge(tp, 4)
                then(v.reduce_max(amax[:, :], by_head(bank[5][0:HD, :]), AX))
                then(v.tensor_tensor(by_head(att[:, :]), by_head(bank[5][0:HD, :]),
                                     amax[:, :].unsqueeze(2).to_broadcast([HD, HEADS, SLICES]), ALU.subtract))
                v.wait_ge(ta, 1)
                then(v.reduce_sum(asum[:, :], by_head(att[:, :]), AX))
                then(v.reciprocal(arec[:, :], asum[:, :]))
                then(v.tensor_tensor(by_head(attn[:, :]), by_head(att[:, :]),
                                     arec[:, :].unsqueeze(2).to_broadcast([HD, HEADS, SLICES]), ALU.mult))
                v.wait_ge(tp, 5)
                then(v.tensor_copy(attT[:, :], bank[0][0:HD, :]))
                v.wait_ge(tp, 6)
                then(v.tensor_copy(oT[:, :], bank[1][0:HD, :]))
                v.wait_ge(tp, 7)
                for q in range(HEADS // 2):
                    then(v.tensor_copy(m_head[:, 2 * q:2 * q + 2, :].rearrange("p h n -> p (h n)"),
                                       bank[2 + q][0:SLICES, :]))
                v.wait_ge(m_in, 32)
                then(v.tensor_copy(MH[:, :, :], M[:, :, :]))
                then(v.tensor_tensor(ML[:, :, :], M[:, :, :], MH[:, :, :].bitcast(F32), ALU.subtract))

            @block.scalar
            def _(act):
                act.wait_ge(tv, 11)
                act.activation(att[:, :], att[:, :], ACT.Exp, scale=SCALE).then_inc(ta, 1)

            @block.sync
            def _(sp):
                sp.wait_ge(tv, 20)
                by_half = m_head[:, :, :].rearrange("p (c a) n -> p c a n", a=2)
                sp.dma_start(M[0:SLICES, :, :], by_half[:, :, 0, :]).then_inc(m_in, 16)
                sp.dma_start(M[SLICES:P, :, :], by_half[:, :, 1, :]).then_inc(m_in, 16)

        with ExitStack() as stage:
            wTg = sb("wTg", [P, 4, TILES * HG], stack=stage)
            x1g = sb("x1g", [P, 4, TILES * D], stack=stage)
            wTH = sb("wTH", [P, 2, TILES * HG], F32R, stack=stage)
            wTL = sb("wTL", [P, 2, TILES * HG], F32R, stack=stage)
            res = sb("res", [P, 2, TILES * D], stack=stage)

            w_in = [sem(f"w_in{i}") for i in range(4)]
            high = sem("wTH_ready")
            low = sem("wTL_ready")
            mixed = sem("w_M_done")
            added = sem("res_ready")
            out_sent = [sem(f"out_sent{i}") for i in range(2)]
            wT_g = wT_s.rearrange("(g a) p n -> g p a n", a=2)
            U = 4
            block = stage.enter_context(nc.Block())

            @block.sync
            def _(sp):
                def step(turn, j):
                    g = turn * U + j
                    if inside(g, GROUPS):
                        at_least(sp, added, 2 * g - 6)
                        sp.dma_start(wTg[:, j, :].rearrange("p (a n) -> p a n", a=2),
                                     wT_g[bass.ds(g, 1)].rearrange("g p a n -> (g p) a n")).then_inc(w_in[j], 16)
                        sp.dma_start(x1g[:, j, :], row(x1_g, g)).then_inc(w_in[j], 16)
                    g = turn * U + j - 2
                    if inside(g, GROUPS):
                        r = j % 2
                        sp.wait_ge(added, 2 * g + 2)
                        if isinstance(g, int) and g == GROUPS - 1:
                            sp.dma_start(out_last, res[0:LAST_ROWS, r, :]).then_inc(out_sent[r], 16)
                        else:
                            sp.dma_start(row(out_g, g), res[:, r, :]).then_inc(out_sent[r], 16)

                run_steps(sp, GROUPS, 2, U, 1, step)
                for i in range(2):
                    sp.wait_ge(out_sent[i], 16 * (GROUPS // 2))

            @block.scalar
            def _(act):
                def step(turn, j):
                    g = turn * U + j
                    if inside(g, GROUPS):
                        act.wait_ge(w_in[j], turn * 32 + 32)
                        at_least(act, mixed, 2 * g - 2)
                        act.activation(wTH[:, j % 2, :], wTg[:, j, :], ACT.Copy).then_inc(high, 1)

                run_steps(act, GROUPS, 0, U, 1, step)

            @block.vector
            def _(v):
                def step(turn, j):
                    g = turn * U + j
                    if inside(g, GROUPS):
                        at_least(v, mixed, 2 * g - 2)
                        v.wait_ge(high, g + 1)
                        v.tensor_tensor(wTL[:, j % 2, :], wTg[:, j, :], wTH[:, j % 2, :].bitcast(F32),
                                        ALU.subtract).then_inc(low, 1)
                    g = turn * U + j - 1
                    if inside(g, GROUPS):
                        r, x_slot = (j - 1) % 2, (j - 1) % 4
                        at_least(v, out_sent[r], (turn * 2 + (j - 1) // 2) * 16)
                        for q in range(2):
                            v.wait_ge(mixed, 2 * g + q + 1)
                            v.tensor_tensor(res[:, r, q * 2 * D:(q + 1) * 2 * D], bank[2 * r + q][:, :],
                                            x1g[:, x_slot, q * 2 * D:(q + 1) * 2 * D], ALU.add).then_inc(added, 1)

                run_steps(v, GROUPS, 1, U, 1, step)

            @block.tensor
            def _(pe):
                def step(turn, j):
                    g = turn * U + j
                    if inside(g, GROUPS):
                        r = j % 2
                        pe.wait_ge(low, g + 1)
                        for q in range(2):
                            at_least(pe, added, 2 * g + q - 3)
                            for t in range(2):
                                to = bank[2 * r + q][:, t * D:(t + 1) * D]
                                pe.matmul(to, ones_bf[:, :], bias_o[:, :], start=True, stop=False)
                                for k in range(HC):
                                    at = slice(((q * 2 + t) * HC + k) * P, ((q * 2 + t) * HC + k + 1) * P)
                                    pe.matmul(to, wTH[:, r, at], ML[:, k, :], start=False, stop=False)
                                    pe.matmul(to, wTL[:, r, at], MH[:, k, :], start=False, stop=False)
                                    last = pe.matmul(to, wTH[:, r, at], MH[:, k, :], start=False,
                                                     stop=(k == HC - 1))
                            last.then_inc(mixed, 1)

                run_steps(pe, GROUPS, 0, U, 1, step)


_INS = ["x", "src", "dst", "L0_gnn_W", "L0_gnn_b", "L0_ffn_W_fx", "L0_ffn_b_fx", "L0_ffn_W_x", "L0_ffn_b_x",
        "L0_ffn_W_slice", "L0_ffn_b_slice", "L0_ffn_W_q", "L0_ffn_W_k", "L0_ffn_W_v", "L0_ffn_W_out",
        "L0_ffn_b_out", "L0_ffn_temperature"]


def kernel(**inputs):
    import numpy as _np
    import concourse.bacc as _bacc
    from concourse import mybir as _mybir
    from concourse.bass_utils import run_bass_kernel_spmd as _run

    nc = _bacc.Bacc("TRN2", target_bir_lowering=False, num_devices=1)
    arrays, args = {}, []
    for name in _INS:
        a = _np.ascontiguousarray(inputs[name])
        arrays[f"in_{name}"] = a
        args.append(nc.dram_tensor(f"in_{name}", a.shape, _mybir.dt.from_np(a.dtype), kind="ExternalInput").ap())
    result = nc.dram_tensor("out_x", (NODES, D), F32, kind="ExternalOutput").ap()
    build(nc, *args, result)
    r = _run(nc, [arrays], core_ids=[0])
    return r.results[0]["out_x"]
```

```python
from contextlib import ExitStack

import concourse.bass as bass
from concourse import mybir

F32 = mybir.dt.float32
F32R = mybir.dt.float32r
BF16 = mybir.dt.bfloat16
I32 = mybir.dt.int32
ALU = mybir.AluOpType
ACT = mybir.ActivationFunctionType
AX = mybir.AxisListType.X

P = 128
D = 256
NODES = 50000
EDGES = 12500
HEADS, HD, SLICES = 8, 64, 64
HG = HEADS * SLICES
KC = D // P
HC = HG // P

TILES = 4
GROUP = P * TILES
GROUPS = -(-NODES // GROUP)
LAST_ROWS = (NODES - (GROUPS - 1) * GROUP) // TILES
assert (NODES - (GROUPS - 1) * GROUP) % TILES == 0
PAIRS = GROUPS * 2
SLOTS2 = 6

CHUNKS = -(-EDGES // P)
SLOTS = CHUNKS * P
TAIL_EDGES = EDGES - (CHUNKS - 1) * P
NO_NODE = 1 << 17
SKIP = 1 << 20

LN_EPS = 1e-5
NORM_EPS = 1e-12
NORM_SHIFT = 1e-5
SCALE = HD ** -0.5


def at_least(engine, sem, value):
    if not isinstance(value, int) or value > 0:
        engine.wait_ge(sem, value)


def run_steps(engine, items, lag, unroll, peel, step, between=()):
    full = items // unroll
    for s in range(peel * unroll):
        step(s // unroll, s % unroll)
        if s in between:
            between[s]()
    with engine.Fori(peel, full) as turn:
        for j in range(unroll):
            step(turn, j)
    for s in range(full * unroll, items + lag):
        step(s // unroll, s % unroll)


def inside(n, total):
    return not isinstance(n, int) or 0 <= n < total


def row(view, n):
    return view[bass.ds(n, 1)].rearrange("a p d -> (a p) d")


def flat(ap):
    return ap.rearrange("p t d -> p (t d)")


def build(nc, x, src, dst, gW, gb, W_fx, b_fx, W_x, b_x, W_slice, b_slice, W_q, W_k, W_v, W_out, b_out,
          temperature, out):
    with ExitStack() as ctx:
        def sb(name, shape, dt=F32, stack=ctx):
            return stack.enter_context(nc.sbuf_tensor(name, shape, dt))

        def sem(name):
            return ctx.enter_context(nc.semaphore(name))

        gated = {nc.gpsimd: sem("pool_gates"), nc.vector: sem("vector_gates"),
                 nc.scalar: sem("scalar_gates")}

        def gate(engine):
            engine.sem_inc(gated[engine], 1)

        ctx.enter_context(nc.allow_non_contiguous_dma("broadcast rows of the small weights"))
        bank = [ctx.enter_context(nc.psum_tensor(f"bank{i}", [P, 512], F32)) for i in range(8)]

        e_src = nc.dram_tensor("e_src", (SLOTS, 1), I32).ap()
        e_dst = nc.dram_tensor("e_dst", (SLOTS + P, 1), I32).ap()
        nbr = nc.dram_tensor("nbr", (GROUPS * GROUP, D), F32).ap()
        x1_s = nc.dram_tensor("x1_s", (GROUPS * GROUP, D), F32).ap()
        wT_s = nc.dram_tensor("wT_s", (PAIRS, P, 2 * HG), F32).ap()

        full = (GROUPS - 1) * GROUP
        x_g = x[0:full].rearrange("(g p j) d -> g p (j d)", p=P, j=TILES)
        x_last = x[full:NODES].rearrange("(p j) d -> p (j d)", j=TILES)
        out_g = out[0:full].rearrange("(g p j) d -> g p (j d)", p=P, j=TILES)
        out_last = out[full:NODES].rearrange("(p j) d -> p (j d)", j=TILES)
        nbr_g = nbr.rearrange("(g p j) d -> g p (j d)", p=P, j=TILES)
        x1_g = x1_s.rearrange("(g p j) d -> g p (j d)", p=P, j=TILES)

        ident = sb("ident", [P, P])
        ident_r = sb("ident_r", [P, P], F32R)
        ones_bf = sb("ones_bf", [P, P], BF16)
        W1H = sb("W1H", [P, KC, D], F32R)
        W1L = sb("W1L", [P, KC, D], F32R)
        W2 = sb("W2", [P, KC, D])
        CH = sb("CH", [P, KC, HG], F32R)
        CL = sb("CL", [P, KC, HG], F32R)
        bias_z = sb("bias_z", [P, D], BF16)
        bo_part = sb("bo_part", [P, D])
        WfxA = sb("WfxA", [P, KC, HG])
        wq = sb("wq", [HD, HD])
        wk = sb("wk", [HD, HD])
        wv = sb("wv", [HD, HD])
        wo = sb("wo", [HD, HEADS, D])
        pick_last = sb("pick_last", [P, P])
        last_row = sb("last_row", [P, 1])
        fill = sb("fill", [P, TILES, D])
        minus_half = sb("minus_half", [P, 6])

        with ExitStack() as stage:
            PIECE = SLOTS // 4
            w1 = sb("w1", [P, KC, D], stack=stage)
            wx = sb("wx", [P, KC, HG], stack=stage)
            wxT = sb("wxT", [HD, HEADS, D], stack=stage)
            wxC = sb("wxC", [HD, HEADS, D + 1], stack=stage)
            hot = sb("hot", [1, P], stack=stage)
            ones_f = sb("ones_f", [P, P], stack=stage)
            ws = sb("ws", [HD, SLICES], stack=stage)
            bxT = sb("bxT", [HD, HEADS], stack=stage)
            bs = sb("bs", [P, SLICES], stack=stage)
            tinv = sb("tinv", [P, HEADS], stack=stage)
            tclip = sb("tclip", [P, HEADS], stack=stage)
            c_f = sb("c_f", [P, KC, HG], stack=stage)
            bo_f = sb("bo_f", [P, D], stack=stage)
            part = sb("part", [P, 3, D], BF16, stack=stage)
            rest = sb("rest", [P, 2, D], stack=stage)
            acc = sb("acc", [P, 2, D], stack=stage)
            wfx_mid = sb("wfx_mid", [P, HG], stack=stage)
            dst_r = sb("dst_r", [CHUNKS, P], I32, stack=stage)
            nxt_r = sb("nxt_r", [CHUNKS, P], I32, stack=stage)
            src_r = sb("src_r", [CHUNKS, P], I32, stack=stage)
            rows_f = sb("rows_f", [CHUNKS, 3, P], stack=stage)
            down = sb("down", [CHUNKS, P], stack=stage)
            down_c = sb("down_c", [CHUNKS, 1], stack=stage)
            flag_f = sb("flag_f", [1, 1], stack=stage)
            flag = sb("flag", [1, 1], I32, stack=stage)
            raw = sb("raw", [P, 2, CHUNKS], stack=stage)
            nxt_c = sb("nxt_c", [P, CHUNKS], stack=stage)
            same = sb("same", [P, CHUNKS], stack=stage)
            tgt_f = sb("tgt_f", [P, CHUNKS], stack=stage)
            all_i = sb("all_i", [P, PIECE], I32, stack=stage)
            all_f = sb("all_f", [P, 4, PIECE], stack=stage)
            place = sb("place", [P, PIECE], stack=stage)
            before = sb("before", [P, PIECE], stack=stage)
            edge_id = sb("edge_id", [P, 4, CHUNKS], stack=stage)
            rank4 = sb("rank4", [P, 4], stack=stage)
            rank_f = sb("rank_f", [P, 1], stack=stage)
            rank_i = sb("rank_i", [P, 1], I32, stack=stage)
            spare = sb("spare", [P, 2], stack=stage)
            moved = sb("moved", [P, 2], I32, stack=stage)
            small = sem("small_weights_in")
            big = sem("big_weights_in")
            bfx_in = sem("bfx_in")
            edges_in = sem("edges_in")
            filled = sem("pads_filled")
            kept = sem("edges_kept")
            again = sem("sorted_edges_in")
            consts = sem("constants_set")
            selected = sem("constants_selected")
            wx_turned = sem("wx_turned")
            wx_copied = sem("wx_copied")
            wx_centred = sem("wx_centred")
            banks_read = sem("c_banks_read")
            c_done = sem("c_done")
            step = sem("vector_step")
            fx_sub = sem("wfx_less_middle")
            down_ready = sem("down_ready")
            down_turned = sem("down_turned")
            flag_ready = sem("flag_ready")
            raw_rows = sem("raw_rows")
            raw_turned = sem("raw_turned")
            raw_ready = sem("raw_columns")
            sorted_rows = sem("sorted_rows")
            sorted_turned = sem("sorted_turned")
            order_done = sem("order_done")
            all_in = sem("all_dst_in")
            ranked = sem("ranked")
            scattered = sem("scattered")
            fall_iota = sem("places_set")
            counted = sem("rank_steps")
            chunks_scattered = sem("chunks_scattered")


            key_col = sb("key_col", [P, CHUNKS], stack=stage)
            keys = sb("keys", [P, CHUNKS, 2], stack=stage)
            src_i = sb("src_i", [P, CHUNKS], I32, stack=stage)
            tgt_i = sb("tgt_i", [P, CHUNKS], I32, stack=stage)
            need_f = sb("need_f", [1, CHUNKS], stack=stage)
            need_i = sb("need_i", [1, CHUNKS], I32, stack=stage)
            need = sb("need", [1, 4], I32, stack=stage)
            g_idx = sb("g_idx", [P, 8], I32, stack=stage)
            s_idx = sb("s_idx", [P, 4], I32, stack=stage)
            key = sb("key", [P, 8, 2], stack=stage)
            xg = sb("xg", [P, 8, D], stack=stage)
            e_bn = sb("e_bn", [P, 8, 6], stack=stage)
            e_mv = sb("e_mv", [P, 8, 2], stack=stage)
            e_var = sb("e_var", [P, 8], stack=stage)
            e_rstd = sb("e_rstd", [P, 8], stack=stage)
            xe = sb("xe", [P, 4, D + 2], stack=stage)
            equal = sb("equal", [P, 4, 2, P], stack=stage)
            total = sb("total", [P, 4, D + 2], stack=stage)
            r_count = sb("r_count", [P, 2], stack=stage)
            mean = sb("mean", [P, 2, D], stack=stage)
            meanT = sb("meanT", [P, 2, D], stack=stage)
            product = sb("product", [P, 4, D], stack=stage)

            fill_in = sem("fill_in")
            written = [sem(f"fill_written{i}") for i in range(2)]
            fills_done = sem("fills_done")
            bias_ready = sem("bias_z_ready")
            ones_set = sem("edge_ones_set")
            indexed = sem("gather_index_ready")
            targeted = sem("scatter_index_ready")
            gathered = [sem(f"rows_gathered{i}") for i in range(8)]
            scattered_rows = [sem(f"rows_scattered{i}") for i in range(4)]
            e_stats = sem("edge_bn_stats")
            e_aggr = sem("edge_bn_aggr")
            e_eps = sem("edge_var_eps")
            e_pow = sem("edge_rstd")
            xe_ready = sem("xe_ready")
            spread = sem("keys_spread")
            masks = sem("masks_ready")
            summed = sem("sums_done")
            total_ready = sem("totals_ready")
            count_ready = sem("r_count_ready")
            mean_ready = sem("means_ready")
            mean_turned = sem("means_turned")
            meanT_ready = sem("meanT_ready")
            multiplied = sem("products_done")
            product_ready = sem("products_ready")
            U = 8

            by_chunk = e_dst[0:SLOTS].rearrange("(c i) a -> c (i a)", i=P)
            block = stage.enter_context(nc.Block())

            @block.sync
            def _(sp):
                def edge_rows(tile, source, shift, done):
                    whole = (CHUNKS - 1) * P
                    sp.dma_start(tile[0:CHUNKS - 1, :],
                                 source[shift:whole + shift].rearrange("(c i) -> c i", i=P)).then_inc(done, 16)
                    sp.dma_start(tile[CHUNKS - 1:CHUNKS, 0:TAIL_EDGES - shift],
                                 source[whole + shift:EDGES].rearrange("(c i) -> c i", c=1)).then_inc(done, 16)

                sp.wait_ge(filled, 3)
                edge_rows(dst_r, dst, 0, edges_in)
                edge_rows(nxt_r, dst, 1, edges_in)
                edge_rows(src_r, src, 0, edges_in)
                sp.dma_start(wx[:, :, :], W_x.rearrange("(k p) n -> p k n", p=P)).then_inc(big, 16)
                sp.dma_start(w1[:, :, :], gW[0:D].rearrange("(k p) n -> p k n", p=P)).then_inc(big, 16)
                sp.dma_start(W2[:, :, :], gW[D:2 * D].rearrange("(k p) n -> p k n", p=P)).then_inc(big, 16)

                sp.wait_ge(fill_in, TILES * 16)

                def fill_step(turn, j):
                    if inside(turn * 2 + j - 2, GROUPS):
                        sp.wait_ge(written[j], turn * 16)
                        sp.sem_inc(fills_done, 1)
                    if inside(turn * 2 + j, GROUPS):
                        sp.dma_start(row(nbr_g, turn * 2 + j), flat(fill[:, :, :])).then_inc(written[j], 16)

                run_steps(sp, GROUPS, 2, 2, 1, fill_step)
                for i in range(4):
                    sp.wait_ge(scattered_rows[i], 16 * len(range(i, CHUNKS, 4)))

            @block.scalar
            def _(act):
                for t in range(TILES):
                    act.dma_start(fill[:, t, :], gb.partition_broadcast(P)).then_inc(fill_in, 16)
                act.dma_start(ws[:, :], W_slice).then_inc(small, 16)
                act.dma_start(bxT[:, :], b_x.rearrange("(h d) -> d h", d=HD)).then_inc(small, 16)
                act.dma_start(bs[:, :], b_slice.partition_broadcast(P)).then_inc(small, 16)
                act.dma_start(tinv[:, :], temperature.rearrange("a h b c -> (a h b c)").partition_broadcast(P)).then_inc(small, 16)
                act.dma_start(bo_f[:, :], b_out.partition_broadcast(P)).then_inc(small, 16)
                act.dma_start(WfxA[:, 0, :], W_fx[0:P]).then_inc(small, 16)
                act.dma_start(WfxA[0:P - 1, 1, :], W_fx[P + 1:D]).then_inc(small, 16)
                act.dma_start(WfxA[P - 1:P, 1, :], b_fx.rearrange("(a n) -> a n", a=1)).then_inc(small, 16)
                act.dma_start(wfx_mid[:, :], W_fx[P:P + 1].rearrange("a n -> (a n)").partition_broadcast(P)).then_inc(small, 16)
                act.dma_start(wq[:, :], W_q).then_inc(small, 16)
                act.dma_start(wk[:, :], W_k).then_inc(small, 16)
                act.dma_start(wv[:, :], W_v).then_inc(small, 16)
                act.dma_start(wo[:, :, :], W_out.rearrange("(h d) n -> d h n", d=HD)).then_inc(small, 16)

                for q in range(4):
                    act.wait_ge(wx_turned, q + 1)
                    act.activation(wxT[:, 2 * q:2 * q + 2, :].rearrange("d h c -> d (h c)"), bank[q][0:HD, :],
                                   ACT.Copy).then_inc(wx_copied, 1)

                def step(turn, j):
                    n = turn * U + j - 5
                    if inside(n, CHUNKS):
                        r, m = (j - 5) % 4, (j - 5) % 2
                        at_least(act, mean_ready, n - 3)
                        act.wait_ge(summed, n + 1)
                        act.activation(total[:, r, :], bank[2 + m][:, 0:D + 2], ACT.Copy).then_inc(total_ready, 1)
                    n = turn * U + j - 6
                    if inside(n, CHUNKS):
                        r, m = (j - 6) % 4, (j - 6) % 2
                        at_least(act, mean_turned, n - 1)
                        act.wait_ge(count_ready, n + 1)
                        act.activation(mean[:, m, :], total[:, r, 0:D], ACT.Copy,
                                       scale=r_count[:, m:m + 1]).then_inc(mean_ready, 1)
                    n = turn * U + j - 7
                    if inside(n, CHUNKS):
                        m = (j - 7) % 2
                        at_least(act, multiplied, n - 1)
                        act.wait_ge(mean_turned, n + 1)
                        act.activation(meanT[:, m, :], bank[4 + m][:, 0:D], ACT.Copy).then_inc(meanT_ready, 1)
                    n = turn * U + j - 8
                    if inside(n, CHUNKS):
                        r, m = j % 4, j % 2
                        act.wait_ge(targeted, n + 1)
                        gate(act)
                        groups = act.value_load(need[0:1, r:r + 1], min_val=1, max_val=GROUPS)
                        act.wait_ge(fills_done, groups)
                        act.wait_ge(multiplied, n + 1)
                        act.activation(product[:, r, :], bank[6 + m][:, 0:D], ACT.Copy).then_inc(product_ready, 1)

                run_steps(act, CHUNKS, 8, U, 2, step)

                act.wait_ge(fx_sub, 2)
                act.dma_start(WfxA[P - 1:P, 1, :], b_fx.rearrange("(a n) -> a n", a=1)).then_inc(bfx_in, 16)
                act.wait_ge(small, 13 * 16)
                act.wait_ge(bfx_in, 16)

            @block.gpsimd
            def _(pool):
                pool.memset(dst_r[:, :], NO_NODE).then_inc(filled, 1)
                pool.memset(nxt_r[:, :], NO_NODE).then_inc(filled, 1)
                pool.memset(src_r[:, :], 0).then_inc(filled, 1)
                pool.memset(ident[:, :], 0.0).then_inc(consts, 1)
                pool.memset(pick_last[:, :], 0.0).then_inc(consts, 1)
                pool.memset(last_row[:, :], 0.0).then_inc(consts, 1)
                pool.memset(ones_bf[:, :], 1.0).then_inc(consts, 1)
                pool.memset(minus_half[:, :], -0.5).then_inc(consts, 1)
                pool.memset(ones_f[:, :], 1.0).then_inc(consts, 1)
                pool.memset(hot[0:1, 0:P - 1], 0.0).then_inc(consts, 1)
                pool.memset(hot[0:1, P - 1:P], 1.0).then_inc(consts, 1)
                pool.wait_ge(consts, 8)
                pool.affine_select(out=ident[:, :], in_=ident[:, :], compare_op=ALU.not_equal, fill=1.0,
                                   base=0, pattern=[[-1, P]], channel_multiplier=1).then_inc(selected, 1)
                pool.affine_select(out=pick_last[:, :], in_=pick_last[:, :], compare_op=ALU.not_equal, fill=1.0,
                                   base=1 - P, pattern=[[0, P]], channel_multiplier=1).then_inc(selected, 1)
                pool.affine_select(out=last_row[:, :], in_=last_row[:, :], compare_op=ALU.not_equal, fill=1.0,
                                   base=1 - P, pattern=[[0, 1]], channel_multiplier=1).then_inc(selected, 1)
                pool.wait_ge(flag_ready, 1)
                unsorted = pool.value_load(flag[0:1, 0:1], min_val=0, max_val=1)
                with pool.If(unsorted > 0):
                    pool.dma_start(by_chunk, dst_r[:, :]).then_inc(kept, 16)
                    pool.dma_start(e_src.rearrange("(c i) a -> c (i a)", i=P), src_r[:, :]).then_inc(kept, 16)
                    pool.dma_start(e_dst[SLOTS:SLOTS + P - TAIL_EDGES].rearrange("(c i) a -> c (i a)", c=1),
                                 dst_r[CHUNKS - 1:CHUNKS, TAIL_EDGES:P]).then_inc(kept, 16)
                    pool.wait_ge(kept, 3 * 16)
                    pool.iota(before[:, :], [[1, PIECE]], base=0, channel_multiplier=0,
                              allow_small_or_imprecise_dtypes=True).then_inc(fall_iota, 1)
                    for q in range(4):
                        pool.iota(edge_id[:, q, :], [[P, CHUNKS]], base=-q * PIECE, channel_multiplier=1,
                                  allow_small_or_imprecise_dtypes=True).then_inc(fall_iota, 1)
                    for q in range(4):
                        pool.dma_start(all_i[:, :], e_dst[q * PIECE:(q + 1) * PIECE].rearrange("n a -> (n a)").partition_broadcast(P)).then_inc(all_in, 16)
                        pool.wait_ge(ranked, q + 1)
                    pool.memset(spare[:, 0:1], 0.0).then_inc(chunks_scattered, 1)
                    with pool.Fori(0, CHUNKS) as c:
                        pool.wait_ge(ranked, c + 5)
                        gate(pool)
                        pool.indirect_dma_start(e_dst[0:SLOTS, :], bass.IndirectOffsetOnAxis(ap=rank_i[:, 0:1], axis=0),
                                                moved[:, 0:1], None).then_inc(scattered, 16)
                        pool.indirect_dma_start(e_src, bass.IndirectOffsetOnAxis(ap=rank_i[:, 0:1], axis=0),
                                                moved[:, 1:2], None).then_inc(scattered, 16)
                        pool.wait_ge(scattered, c * 32 + 32)
                        gate(pool)
                        pool.memset(spare[:, 0:1], 0.0).then_inc(chunks_scattered, 1)
                    pool.wait_ge(raw_ready, 1)
                    pool.dma_start(dst_r[:, :], by_chunk).then_inc(again, 16)
                    pool.dma_start(nxt_r[:, :], e_dst[1:SLOTS + 1].rearrange("(c i) a -> c (i a)", i=P)).then_inc(again, 16)
                    pool.dma_start(src_r[:, :], e_src.rearrange("(c i) a -> c (i a)", i=P)).then_inc(again, 16)
                    pool.wait_ge(again, 3 * 16)
                pool.memset(spare[:, 1:2], 0.0).then_inc(order_done, 1)
                pool.memset(xe[:, :, D:D + 1], 1.0).then_inc(ones_set, 1)
                pool.memset(xe[:, :, D + 1:D + 2], 0.0).then_inc(ones_set, 1)

                def step(turn, j):
                    n = turn * U + j
                    if inside(n, CHUNKS):
                        at_least(pool, xe_ready, n - 7)
                        pool.wait_ge(indexed, n + 1)
                        gate(pool)
                        pool.indirect_dma_start(xg[:, j, :], None, x,
                                                bass.IndirectOffsetOnAxis(ap=g_idx[:, j:j + 1], axis=0)
                                                ).then_inc(gathered[j], 16)
                    n = turn * U + j - 3
                    if j % 2 and inside(n, CHUNKS):
                        r = (j - 3) % 8
                        pool.wait_ge(e_eps, n + 2)
                        pool.tensor_tensor(e_rstd[:, r:r + 2], e_var[:, r:r + 2], minus_half[:, 0:2],
                                           ALU.pow).then_inc(e_pow, 1)
                    n = turn * U + j - 9
                    if inside(n, CHUNKS):
                        r = (j - 9) % 4
                        pool.wait_ge(product_ready, n + 1)
                        gate(pool)
                        pool.indirect_dma_start(nbr, bass.IndirectOffsetOnAxis(ap=s_idx[:, r:r + 1], axis=0),
                                                product[:, r, :], None, bounds_check=NODES - 1,
                                                oob_is_err=False).then_inc(scattered_rows[r], 16)

                run_steps(pool, CHUNKS, 9, U, 2, step)

            @block.vector
            def _(v):
                done = [0]

                def then(instruction):
                    instruction.then_inc(step, 1)
                    done[0] += 1
                    v.wait_ge(step, done[0])

                def split_bias(b_f, b_rows):
                    then(v.tensor_copy(part[:, 0, :], b_f))
                    then(v.tensor_tensor(rest[:, 0, :], b_f, part[:, 0, :], ALU.subtract))
                    then(v.tensor_copy(part[:, 1, :], rest[:, 0, :]))
                    then(v.tensor_tensor(rest[:, 1, :], rest[:, 0, :], part[:, 1, :], ALU.subtract))
                    then(v.tensor_copy(part[:, 2, :], rest[:, 1, :]))
                    then(v.tensor_scalar(acc[:, 0, :], part[:, 0, :], ident[:, 0:1], None, ALU.mult))
                    then(v.scalar_tensor_tensor(acc[:, 1, :], part[:, 1, :], ident[:, 1:2], acc[:, 0, :],
                                                ALU.mult, ALU.add))
                    return v.scalar_tensor_tensor(b_rows[:, :], part[:, 2, :], ident[:, 2:3], acc[:, 1, :],
                                                  ALU.mult, ALU.add)

                v.wait_ge(edges_in, 6 * 16)
                v.tensor_copy(rows_f[:, 0, :], dst_r[:, :])
                v.tensor_copy(rows_f[:, 1, :], src_r[:, :]).then_inc(raw_rows, 1)
                then(v.tensor_copy(rows_f[:, 2, :], nxt_r[:, :]))
                then(v.tensor_tensor(down[:, :], rows_f[:, 2, :], rows_f[:, 0, :], ALU.is_lt))
                v.reduce_max(down_c[:, :], down[:, :], AX).then_inc(down_ready, 1)
                v.wait_ge(down_turned, 1)
                then(v.reduce_max(flag_f[:, :], bank[7][0:1, 0:CHUNKS], AX))
                v.tensor_copy(flag[:, :], flag_f[:, :]).then_inc(flag_ready, 1)
                v.wait_ge(raw_turned, 1)
                v.tensor_copy(raw[:, 0, :], bank[4][:, 0:CHUNKS]).then_inc(raw_ready, 1)
                then(v.tensor_copy(raw[:, 1, :], bank[4][:, P:P + CHUNKS]))
                v.wait_ge(flag_ready, 1)
                unsorted = v.value_load(flag[0:1, 0:1], min_val=0, max_val=1)
                with v.If(unsorted > 0):
                    for q in range(4):
                        v.wait_ge(all_in, 16 * (q + 1))
                        v.tensor_copy(all_f[:, q, :], all_i[:, :]).then_inc(ranked, 1)
                    v.wait_ge(fall_iota, 5)
                    v.wait_ge(ranked, 4)
                    with v.Fori(0, CHUNKS) as c:
                        for q in range(4):
                            v.tensor_scalar(place[:, :], before[:, :], edge_id[:, q, bass.ds(c, 1)], -0.5,
                                            ALU.is_lt, ALU.mult).then_inc(counted, 1)
                            v.wait_ge(counted, c * 13 + 3 * q + 1)
                            v.tensor_tensor(place[:, :], place[:, :], all_f[:, q, :], ALU.add).then_inc(counted, 1)
                            v.wait_ge(counted, c * 13 + 3 * q + 2)
                            v.tensor_scalar(place[:, :], place[:, :], raw[:, 0, bass.ds(c, 1)], 0.0,
                                            ALU.is_lt, ALU.add, accum_out=rank4[:, q:q + 1]).then_inc(counted, 1)
                            v.wait_ge(counted, c * 13 + 3 * q + 3)
                        v.reduce_sum(rank_f[:, :], rank4[:, :], AX).then_inc(counted, 1)
                        v.wait_ge(counted, c * 13 + 13)
                        v.wait_ge(chunks_scattered, c + 1)
                        gate(v)
                        v.tensor_copy(moved[:, 0:1], raw[:, 0, bass.ds(c, 1)])
                        v.tensor_copy(moved[:, 1:2], raw[:, 1, bass.ds(c, 1)])
                        v.tensor_copy(rank_i[:, :], rank_f[:, :]).then_inc(ranked, 1)

                v.wait_ge(selected, 3)
                v.wait_ge(order_done, 1)
                v.tensor_copy(rows_f[:, 0, :], dst_r[:, :])
                v.tensor_copy(rows_f[:, 1, :], src_r[:, :])
                v.tensor_copy(rows_f[:, 2, :], nxt_r[:, :]).then_inc(sorted_rows, 1)
                v.wait_ge(sorted_turned, 1)
                v.tensor_copy(src_i[:, :], bank[5][:, P:P + CHUNKS])
                v.tensor_copy(keys[:, :, 0], bank[5][:, 0:CHUNKS])
                v.memset(keys[:, 0:1, 1], 0.0)
                v.tensor_copy(key_col[:, :], bank[5][:, 0:CHUNKS])
                v.tensor_scalar(need_f[:, :], bank[7][0:1, P:P + CHUNKS], 1.0 / GROUP, 1.5, ALU.mult, ALU.add)
                then(v.tensor_copy(nxt_c[:, :], bank[5][:, 2 * P:2 * P + CHUNKS]))
                v.tensor_tensor(same[:, :], nxt_c[:, :], key_col[:, :], ALU.is_equal)
                v.tensor_scalar(need_f[:, :], need_f[:, :], float(GROUPS), None, ALU.min)
                then(v.tensor_scalar(keys[:, 1:CHUNKS, 1], key_col[:, 0:CHUNKS - 1], 1.0, last_row[:, 0:1],
                                     ALU.add, ALU.mult))
                v.tensor_copy(need_i[:, :], need_f[:, :])
                v.tensor_scalar(keys[:, :, 1], keys[:, :, 1], -1.0, None, ALU.add)
                then(v.scalar_tensor_tensor(tgt_f[:, :], same[:, :], float(SKIP), key_col[:, :], ALU.mult, ALU.add))
                then(v.tensor_copy(tgt_i[:, :], tgt_f[:, :]))

                def edge_step(turn, j):
                    n = turn * U + j
                    if inside(n, CHUNKS):
                        at_least(v, gathered[j], turn * 16)
                        gate(v)
                        v.tensor_copy(key[:, j, :], keys[:, bass.ds(n, 1), :].rearrange("p a b -> p (a b)"))
                        v.tensor_copy(g_idx[:, j:j + 1], src_i[:, bass.ds(n, 1)]).then_inc(indexed, 1)
                    n = turn * U + j - 2
                    if inside(n, CHUNKS):
                        r = (j - 2) % 8
                        v.wait_ge(gathered[r], (turn + (j - 2) // 8) * 16 + 16)
                        v.bn_stats(e_bn[:, r, :], xg[:, r, :]).then_inc(e_stats, 1)
                    n = turn * U + j - 3
                    if inside(n, CHUNKS):
                        q, m = (j - 3) % 4, (j - 3) % 2
                        v.wait_ge(spread, n + 1)
                        at_least(v, summed, n - 3)
                        v.tensor_tensor(equal[:, q, :, :], bank[m][:, 0:P].unsqueeze(1).to_broadcast([P, 2, P]),
                                        key[:, (j - 3) % 8, :].unsqueeze(2).to_broadcast([P, 2, P]),
                                        ALU.is_equal).then_inc(masks, 1)
                    n = turn * U + j - 2
                    if inside(n, CHUNKS):
                        r = (j - 2) % 8
                        v.wait_ge(e_stats, n + 1)
                        gate(v)
                        v.bn_aggr(e_mv[:, r, :], e_bn[:, r, :]).then_inc(e_aggr, 1)
                    n = turn * U + j - 6
                    if inside(n, CHUNKS):
                        r, m = (j - 6) % 4, (j - 6) % 2
                        at_least(v, mean_ready, n - 1)
                        v.wait_ge(total_ready, n + 1)
                        v.reciprocal(r_count[:, m:m + 1], total[:, r, D:D + 1]).then_inc(count_ready, 1)
                    n = turn * U + j - 2
                    if inside(n, CHUNKS):
                        r = (j - 2) % 8
                        v.wait_ge(e_aggr, n + 1)
                        v.tensor_scalar(e_var[:, r:r + 1], e_mv[:, r, 1:2], LN_EPS, None, ALU.add).then_inc(e_eps, 1)
                    n = turn * U + j - 4
                    if inside(n, CHUNKS):
                        r, r8 = (j - 4) % 4, (j - 4) % 8
                        at_least(v, summed, n - 3)
                        v.wait_ge(e_pow, turn * 4 + (j - 4) // 2 + 1)
                        gate(v)
                        v.tensor_scalar(xe[:, r, 0:D], xg[:, r8, :], e_mv[:, r8, 0:1], e_rstd[:, r8:r8 + 1],
                                        ALU.subtract, ALU.mult).then_inc(xe_ready, 1)
                    n = turn * U + j - 8
                    if inside(n, CHUNKS):
                        r = j % 4
                        at_least(v, scattered_rows[r], (turn * 2 + (j - 8) // 4) * 16)
                        gate(v)
                        v.tensor_copy(need[:, r:r + 1], need_i[:, bass.ds(n, 1)])
                        v.tensor_copy(s_idx[:, r:r + 1], tgt_i[:, bass.ds(n, 1)]).then_inc(targeted, 1)

                def part_bias():
                    v.wait_ge(fill_in, TILES * 16)
                    split_bias(fill[:, 0, :], bias_z).then_inc(bias_ready, 1)

                def part_centre():
                    v.wait_ge(small, 13 * 16)
                    v.wait_ge(wx_copied, 4)
                    v.tensor_copy(wxC[:, :, D], bxT[:, :])
                    v.tensor_tensor(wxC[:, :, 0:D], wxT[:, :, :], wxT[:, :, P:P + 1].to_broadcast([HD, HEADS, D]),
                                    ALU.subtract).then_inc(wx_centred, 1)
                    v.tensor_scalar(bo_part[:, :], bo_f[:, :], 1.0 / HEADS, None, ALU.mult)
                    then(v.tensor_scalar(tclip[:, :], tinv[:, :], 0.1, 5.0, ALU.max, ALU.min))
                    then(v.reciprocal(tinv[:, :], tclip[:, :]))

                def part_scale():
                    v.wait_ge(c_done, 1)
                    for k in range(KC):
                        v.tensor_tensor(c_f[:, k, :].rearrange("p (h g) -> p h g", h=HEADS),
                                        bank[4 + k][:, :].rearrange("p (h g) -> p h g", h=HEADS),
                                        tinv[:, :].unsqueeze(2).to_broadcast([P, HEADS, SLICES]), ALU.mult)
                    for k in range(KC):
                        last = v.scalar_tensor_tensor(w1[:, k, :], bank[6][:, 0:D], -1.0 / D, w1[:, k, :],
                                                      ALU.mult, ALU.add)
                    then(last)
                    v.sem_inc(banks_read, 1)

                def part_high():
                    v.tensor_copy(ident_r[:, :], ident[:, :])
                    v.tensor_copy(W1H[:, :, :], w1[:, :, :])
                    then(v.tensor_copy(CH[:, :, :], c_f[:, :, :]))

                def part_low():
                    v.tensor_tensor(W1L[:, :, :], w1[:, :, :], W1H[:, :, :].bitcast(F32), ALU.subtract)
                    v.tensor_tensor(CL[:, :, :], c_f[:, :, :], CH[:, :, :].bitcast(F32), ALU.subtract)

                def part_fx():
                    for k in range(KC):
                        v.tensor_tensor(WfxA[:, k, :], WfxA[:, k, :], wfx_mid[:, :], ALU.subtract).then_inc(fx_sub, 1)

                run_steps(v, CHUNKS, 8, U, 2, edge_step, {3: part_centre, 5: part_bias, 6: part_scale, 9: part_high,
                                                          11: part_low, 13: part_fx})

            @block.tensor
            def _(pe):
                pe.wait_ge(selected, 3)
                pe.wait_ge(raw_rows, 1)
                for i in range(2):
                    last = pe.transpose(bank[4][:, i * P:i * P + CHUNKS], rows_f[:, i, :], ident[0:CHUNKS, 0:CHUNKS])
                last.then_inc(raw_turned, 1)
                pe.wait_ge(down_ready, 1)
                pe.transpose(bank[7][0:1, 0:CHUNKS], down_c[:, :], ident[0:CHUNKS, 0:CHUNKS]).then_inc(down_turned, 1)
                pe.wait_ge(sorted_rows, 1)
                for i in range(3):
                    pe.transpose(bank[5][:, i * P:i * P + CHUNKS], rows_f[:, i, :], ident[0:CHUNKS, 0:CHUNKS])
                pe.transpose(bank[7][0:1, P:P + CHUNKS], rows_f[:, 0, P - 1:P],
                             ident[0:CHUNKS, 0:CHUNKS]).then_inc(sorted_turned, 1)
                pe.wait_ge(big, 3 * 16)
                for h in range(HEADS):
                    for k in range(KC):
                        last = pe.transpose(bank[h // 2][0:HD, (h % 2) * D + k * P:(h % 2) * D + (k + 1) * P],
                                            wx[:, k, h * HD:(h + 1) * HD], ident[:, :])
                    if h % 2:
                        last.then_inc(wx_turned, 1)
                pe.wait_ge(wx_copied, 4)
                pe.wait_ge(ones_set, 2)

                def step(turn, j):
                    n = turn * U + j - 5
                    if inside(n, CHUNKS):
                        r, m = (j - 5) % 4, (j - 5) % 2
                        first = isinstance(n, int) and n == 0
                        at_least(pe, total_ready, n)
                        pe.wait_ge(masks, n + 1)
                        pe.wait_ge(xe_ready, n + 1)
                        last = pe.matmul(bank[2 + m][:, 0:D + 2], equal[:, r, 0, :], xe[:, r, :], start=True, stop=first)
                        if not first:
                            last = pe.matmul(bank[2 + m][:, 0:D + 2], equal[:, r, 1, :], total[:, (j - 6) % 4, :],
                                             start=False, stop=True)
                        last.then_inc(summed, 1)
                    n = turn * U + j - 2
                    if inside(n, CHUNKS):
                        pe.wait_ge(indexed, n + 1)
                        at_least(pe, masks, n - 1)
                        pe.matmul(bank[(j - 2) % 2][:, 0:P], key[:, (j - 2) % 8, 0:1].to_broadcast([P, P]), ident[:, :],
                                  start=True, stop=True).then_inc(spread, 1)
                    n = turn * U + j - 7
                    if inside(n, CHUNKS):
                        m = (j - 7) % 2
                        pe.wait_ge(mean_ready, n + 1)
                        at_least(pe, meanT_ready, n - 1)
                        for k in range(KC):
                            last = pe.transpose(bank[4 + m][:, k * P:(k + 1) * P], mean[:, m, k * P:(k + 1) * P],
                                                ident[:, :])
                        last.then_inc(mean_turned, 1)
                    n = turn * U + j - 8
                    if inside(n, CHUNKS):
                        m = j % 2
                        pe.wait_ge(meanT_ready, n + 1)
                        at_least(pe, product_ready, n - 1)
                        pe.matmul(bank[6 + m][:, 0:D], ones_bf[:, :], bias_z[:, :], start=True, stop=False)
                        for k in range(KC):
                            last = pe.matmul(bank[6 + m][:, 0:D], meanT[:, m, k * P:(k + 1) * P], W2[:, k, :],
                                             start=False, stop=(k == KC - 1))
                        last.then_inc(multiplied, 1)

                def part_c():
                    pe.wait_ge(wx_centred, 1)
                    pe.wait_ge(small, 13 * 16)
                    for k in range(KC):
                        pe.matmul(bank[6][:, 0:D], ones_f[:, :], w1[:, k, :], start=(k == 0), stop=(k == KC - 1))
                    for h in range(HEADS):
                        cols = slice(h * SLICES, (h + 1) * SLICES)
                        pe.matmul(bank[4][:, cols], wxC[:, h, 0:P], ws[:, :], start=True, stop=True)
                        pe.matmul(bank[5][:, cols], wxC[:, h, P + 1:D + 1], ws[:, :], start=True, stop=False)
                        last = pe.matmul(bank[5][:, cols], hot[0:1, :], bs[0:1, :], start=False, stop=True)
                    last.then_inc(c_done, 1)

                def part_free():
                    pe.wait_ge(banks_read, 1)
                    pe.wait_ge(bias_ready, 1)

                run_steps(pe, CHUNKS, 8, U, 2, step, {4: part_c, 6: part_free})

        with ExitStack() as stage:
            xs = sb("xs", [P, 4, TILES, D], stack=stage)
            ns = sb("ns", [P, 4, TILES, D], stack=stage)
            bn1 = sb("bn1", [P, 2, 2, 6], stack=stage)
            mv1 = sb("mv1", [P, 2, 2, 2], stack=stage)
            xH = sb("xH", [P, 2, 2 * D], F32R, stack=stage)
            xL = sb("xL", [P, 2, 2 * D], F32R, stack=stage)
            xTH = sb("xTH", [P, 2, 2 * D], F32R, stack=stage)
            xTL = sb("xTL", [P, 2, 2 * D], F32R, stack=stage)
            z = sb("z", [P, 2, 2 * D], stack=stage)
            relu = sb("relu", [P, 4, 2 * D], stack=stage)
            square = sb("square", [P, 2 * D], stack=stage)
            norm2 = sb("norm2", [P, 2, 2], stack=stage)
            squares = sb("squares", [P, 2, 6], stack=stage)
            roots = sb("roots", [P, 4, 6], stack=stage)
            x1 = sb("x1", [P, 4, TILES, D], stack=stage)
            bn2 = sb("bn2", [P, 2, 2, 6], stack=stage)
            mv2 = sb("mv2", [P, 2, 2, 2], stack=stage)
            y = sb("y", [P, 2, 2, D], stack=stage)
            yH = sb("yH", [P, 8, 2, D + 1], F32R, stack=stage)
            yL = sb("yL", [P, 8, 2, D + 1], F32R, stack=stage)
            yTH = sb("yTH", [P, 2, 2 * D], F32R, stack=stage)
            yTL = sb("yTL", [P, 2, 2 * D], F32R, stack=stage)
            top = sb("top", [P, 2, 2 * HEADS], stack=stage)
            e = sb("e", [P, 2, 2 * HG], stack=stage)
            esum = sb("esum", [P, 2, 2 * HEADS], stack=stage)
            erec = sb("erec", [P, 2, 2 * HEADS], stack=stage)
            w = sb("w", [P, 2, 2 * HG], stack=stage)
            wH = sb("wH", [P, 2, 2 * HG], F32R, stack=stage)
            wL = sb("wL", [P, 2, 2 * HG], F32R, stack=stage)
            wT = sb("wT", [P, 4, 2 * HG], stack=stage)
            zero_bf = sb("zero_bf", [P, HG], BF16, stack=stage)

            x_in = [sem(f"x_in{i}") for i in range(4)]
            x1_out = [sem(f"x1_out{i}") for i in range(4)]
            wT_out = [sem(f"wT_out{i}") for i in range(4)]
            ones_y = sem("y_ones_set")
            squares_set = sem("squares_set")
            stats1 = sem("stats1")
            aggr1 = sem("aggr1")
            var1_ready = sem("var1_ready")
            xH_ready = sem("xH_ready")
            xL_ready = sem("xL_ready")
            x_turned = sem("x_turned")
            xT_ready = sem("xT_ready")
            z_done = sem("z_done")
            z_ready = sem("z_ready")
            relu_ready = sem("relu_ready")
            norm2_ready = sem("norm2_ready")
            norm2c_ready = sem("norm2c_ready")
            x1_ready = sem("x1_ready")
            stats2 = sem("stats2")
            aggr2 = sem("aggr2")
            var2_ready = sem("var2_ready")
            roots_ready = sem("roots_ready")
            y_ready = sem("y_ready")
            yH_ready = sem("yH_ready")
            yL_ready = sem("yL_ready")
            y_turned = sem("y_turned")
            yT_ready = sem("yT_ready")
            logits_done = sem("logits_done")
            top_ready = sem("top_ready")
            shifted = sem("logits_shifted")
            exp_ready = sem("exp_ready")
            esum_ready = sem("esum_ready")
            erec_ready = sem("erec_ready")
            w_ready = sem("w_ready")
            wH_ready = sem("wH_ready")
            wL_ready = sem("wL_ready")
            w_turned = sem("w_turned")
            wT_ready = sem("wT_ready")
            sums_in = sem("token_sums_in")

            NORM, VAR1, VAR2 = slice(0, 2), slice(2, 4), slice(4, 6)
            BTH, BTL, BZ, BL, BW, BS = 0, 1, 2, 3, 5, 6
            U = 8
            LAG = 8
            block = stage.enter_context(nc.Block())

            def heads(ap):
                return ap.rearrange("p (h g) -> p h g", g=SLICES)

            @block.sync
            def _(sp):
                def step(turn, j):
                    g = turn * U + j
                    if inside(g, GROUPS):
                        r = j % 4
                        at_least(sp, x1_ready, 2 * g - 6)
                        if isinstance(g, int) and g == GROUPS - 1:
                            sp.dma_start(flat(xs[0:LAST_ROWS, r]), x_last).then_inc(x_in[r], 16)
                        else:
                            sp.dma_start(flat(xs[:, r]), row(x_g, g)).then_inc(x_in[r], 16)
                        sp.dma_start(flat(ns[:, r]), row(nbr_g, g)).then_inc(x_in[r], 16)
                    g = turn * U + j - 3
                    if inside(g, GROUPS):
                        r = (j - 3) % 4
                        sp.wait_ge(x1_ready, 2 * g + 2)
                        sp.dma_start(row(x1_g, g), flat(x1[:, r])).then_inc(x1_out[r], 16)
                    for t in range(2):
                        n = (turn * U + j - 5) * 2 + t
                        if inside(n, PAIRS):
                            r = ((j - 5) * 2 + t) % 4
                            sp.wait_ge(wT_ready, 2 * n + 2)
                            sp.dma_start(row(wT_s, n), wT[:, r, :]).then_inc(wT_out[r], 16)

                run_steps(sp, GROUPS, 5, U, 1, step)
                for i in range(4):
                    sp.wait_ge(x1_out[i], 16 * len(range(i, GROUPS, 4)))
                    sp.wait_ge(wT_out[i], 16 * len(range(i, PAIRS, 4)))

            @block.gpsimd
            def _(pool):
                pool.memset(yH[:, :, :, D:D + 1].bitcast(F32), 1.0).then_inc(ones_y, 1)
                pool.memset(yL[:, :, :, D:D + 1].bitcast(F32), 0.0).then_inc(ones_y, 1)
                pool.memset(zero_bf[:, :], 0.0).then_inc(ones_y, 1)

                def step(turn, j):
                    n = turn * U + j - 5
                    if inside(n, PAIRS):
                        pool.wait_ge(yH_ready, n + 1)
                        pool.tensor_tensor(yL[:, (j - 5) % 8, :, 0:D], y[:, (j - 5) % 2, :, :],
                                           yH[:, (j - 5) % 8, :, 0:D].bitcast(F32), ALU.subtract).then_inc(yL_ready, 1)
                    n = turn * U + j
                    if inside(n, PAIRS):
                        r, gslot, t0 = j % 2, (j // 2) % 4, (j % 2) * 2
                        at_least(pool, x_turned, n - 1)
                        pool.wait_ge(xH_ready, n + 1)
                        pool.tensor_tensor(xL[:, r, :], flat(xs[:, gslot, t0:t0 + 2]), xH[:, r, :].bitcast(F32),
                                           ALU.subtract).then_inc(xL_ready, 1)
                    n = turn * U + j - 7
                    if inside(n, PAIRS):
                        r = (j - 7) % 2
                        at_least(pool, wL_ready, n - 1)
                        pool.wait_ge(erec_ready, n + 1)
                        pool.tensor_tensor(heads(w[:, r, :]), heads(e[:, r, :]),
                                           erec[:, r, :].unsqueeze(2).to_broadcast([P, 2 * HEADS, SLICES]),
                                           ALU.mult).then_inc(w_ready, 1)
                    s = turn * U + j
                    if inside(s - 4, PAIRS) or inside(s, PAIRS):
                        if inside(s, PAIRS):
                            pool.wait_ge(var1_ready, s + 1)
                        if inside(s - 3, PAIRS):
                            pool.wait_ge(norm2c_ready, s - 2)
                        if inside(s - 4, PAIRS):
                            pool.wait_ge(var2_ready, s - 3)
                        pool.tensor_tensor(roots[:, j % 4, :], squares[:, j % 2, :], minus_half[:, 0:6],
                                           ALU.pow).then_inc(roots_ready, 1)
                    n = turn * U + j - 7
                    if inside(n, PAIRS):
                        r = (j - 7) % 2
                        at_least(pool, sums_in, n - 1)
                        pool.wait_ge(wH_ready, n + 1)
                        pool.tensor_tensor(wL[:, r, :], w[:, r, :], wH[:, r, :].bitcast(F32),
                                           ALU.subtract).then_inc(wL_ready, 1)

                run_steps(pool, PAIRS, LAG, U, 2, step)

            @block.vector
            def _(v):
                v.memset(squares[:, :, :], 1.0).then_inc(squares_set, 1)
                v.wait_ge(squares_set, 1)

                def step(turn, j):
                    n = turn * U + j - 3
                    if inside(n, PAIRS):
                        at_least(v, roots_ready, n + 2)
                        v.wait_ge(norm2_ready, n + 1)
                        v.tensor_scalar(squares[:, j % 2, NORM], norm2[:, (j - 3) % 2, :], NORM_EPS * NORM_EPS, None,
                                        ALU.max).then_inc(norm2c_ready, 1)
                    n = turn * U + j - 5
                    if inside(n, PAIRS):
                        r, gslot, t0 = (j - 5) % 2, ((j - 5) // 2) % 4, ((j - 5) % 2) * 2
                        at_least(v, yL_ready, n - 1)
                        v.wait_ge(roots_ready, n + 5)
                        gate(v)
                        for t in range(2):
                            last = v.tensor_scalar(y[:, r, t, :], x1[:, gslot, t0 + t, :], mv2[:, r, t, 0:1],
                                                   roots[:, (j - 1) % 4, 4 + t:5 + t], ALU.subtract, ALU.mult)
                        last.then_inc(y_ready, 1)
                    n = turn * U + j - 2
                    if inside(n, PAIRS):
                        r, gslot, t0 = (j - 2) % 2, ((j - 2) // 2) % 4, ((j - 2) % 2) * 2
                        at_least(v, relu_ready, n - 1)
                        v.wait_ge(roots_ready, n + 1)
                        v.wait_ge(z_done, n + 1)
                        gate(v)
                        for t in range(2):
                            last = v.scalar_tensor_tensor(z[:, r, t * D:(t + 1) * D], bank[BZ][:, t * D:(t + 1) * D],
                                                          roots[:, (j - 2) % 4, 2 + t:3 + t],
                                                          ns[:, gslot, t0 + t, :], ALU.mult, ALU.add)
                        last.then_inc(z_ready, 1)
                    n = turn * U + j
                    if inside(n, PAIRS):
                        r, gslot, t0 = j % 2, (j // 2) % 4, (j % 2) * 2
                        v.wait_ge(x_in[gslot], turn * 32 + 32)
                        for t in range(2):
                            last = v.bn_stats(bn1[:, r, t, :], xs[:, gslot, t0 + t, :])
                        last.then_inc(stats1, 1)
                        v.wait_ge(stats1, n + 1)
                        gate(v)
                        for t in range(2):
                            last = v.bn_aggr(mv1[:, r, t, :], bn1[:, r, t, :])
                        last.then_inc(aggr1, 1)
                        v.wait_ge(aggr1, n + 1)
                        at_least(v, roots_ready, n - 1)
                        v.tensor_scalar(squares[:, j % 2, VAR1], mv1[:, r, :, 1], LN_EPS, None, ALU.add).then_inc(var1_ready, 1)
                    n = turn * U + j - 7
                    if inside(n, PAIRS):
                        r = (j - 7) % 2
                        v.wait_ge(exp_ready, n + 1)
                        v.reduce_sum(esum[:, r, :], heads(e[:, r, :]), AX).then_inc(esum_ready, 1)
                        at_least(v, w_ready, n - 1)
                        v.wait_ge(esum_ready, n + 1)
                        v.reciprocal(erec[:, r, :], esum[:, r, :]).then_inc(erec_ready, 1)
                    n = turn * U + j - 4
                    if inside(n, PAIRS):
                        r, gslot, t0 = (j - 4) % 2, ((j - 4) // 2) % 4, ((j - 4) % 2) * 2
                        v.wait_ge(roots_ready, n + 4)
                        if (j - 4) % 2 == 0:
                            at_least(v, x1_out[gslot], (turn + (j - 4) // 8) * 16)
                        for t in range(2):
                            last = v.scalar_tensor_tensor(x1[:, gslot, t0 + t, :],
                                                          relu[:, (j - 4) % 4, t * D:(t + 1) * D],
                                                          roots[:, (j - 1) % 4, t:t + 1], xs[:, gslot, t0 + t, :],
                                                          ALU.mult, ALU.add)
                        last.then_inc(x1_ready, 1)
                        v.wait_ge(x1_ready, n + 1)
                        for t in range(2):
                            last = v.bn_stats(bn2[:, r, t, :], x1[:, gslot, t0 + t, :])
                        last.then_inc(stats2, 1)
                        v.wait_ge(stats2, n + 1)
                        gate(v)
                        for t in range(2):
                            last = v.bn_aggr(mv2[:, r, t, :], bn2[:, r, t, :])
                        last.then_inc(aggr2, 1)
                        v.wait_ge(aggr2, n + 1)
                        v.tensor_scalar(squares[:, j % 2, VAR2], mv2[:, r, :, 1], LN_EPS, None, ALU.add).then_inc(var2_ready, 1)
                    n = turn * U + j - 6
                    if inside(n, PAIRS):
                        r = (j - 6) % 2
                        at_least(v, w_ready, n - 1)
                        for t in range(2):
                            v.wait_ge(logits_done, 2 * n + t + 1)
                            v.reduce_max(top[:, r, t * HEADS:(t + 1) * HEADS], heads(bank[BL + t][:, :]),
                                         AX).then_inc(top_ready, 1)
                            v.wait_ge(top_ready, 2 * n + t + 1)
                            v.tensor_tensor(heads(e[:, r, t * HG:(t + 1) * HG]), heads(bank[BL + t][:, :]),
                                            top[:, r, t * HEADS:(t + 1) * HEADS].unsqueeze(2).to_broadcast([P, HEADS, SLICES]),
                                            ALU.subtract).then_inc(shifted, 1)

                run_steps(v, PAIRS, LAG, U, 2, step)

            @block.scalar
            def _(act):
                def step(turn, j):
                    def w_out(t):
                        n = turn * U + j - 8
                        if inside(n, PAIRS):
                            r = j % 4
                            if t == 0:
                                at_least(act, wT_out[r], (turn * 2 + (j - 8) // 4) * 16)
                            act.wait_ge(w_turned, 2 * n + t + 1)
                            act.activation(wT[:, r, t * HG:(t + 1) * HG], bank[BW][:, :], ACT.Copy).then_inc(wT_ready, 1)

                    n = turn * U + j - 1
                    if inside(n, PAIRS):
                        r = (j - 1) % 2
                        at_least(act, z_done, n - 1)
                        act.wait_ge(x_turned, n + 1)
                        act.activation(xTH[:, r, :], bank[BTH][:, :], ACT.Copy)
                        act.activation(xTL[:, r, :], bank[BTL][:, :], ACT.Copy).then_inc(xT_ready, 1)
                    n = turn * U + j - 5
                    if inside(n, PAIRS):
                        at_least(act, sums_in, n - 7)
                        act.wait_ge(y_ready, n + 1)
                        act.activation(yH[:, (j - 5) % 8, :, 0:D], y[:, (j - 5) % 2, :, :], ACT.Copy).then_inc(yH_ready, 1)
                    n = turn * U + j - 2
                    if inside(n, PAIRS):
                        r, q = (j - 2) % 2, (j - 2) % 4
                        at_least(act, x1_ready, n - 3)
                        act.wait_ge(z_ready, n + 1)
                        act.activation(relu[:, q, :], z[:, r, :], ACT.Relu).then_inc(relu_ready, 1)
                        at_least(act, norm2c_ready, n - 1)
                        act.wait_ge(relu_ready, n + 1)
                        at_least(act, norm2_ready, n)
                        for t in range(2):
                            last = act.activation(square[:, t * D:(t + 1) * D], relu[:, q, t * D:(t + 1) * D],
                                                  ACT.Square, accum_out=norm2[:, r, t:t + 1])
                        last.then_inc(norm2_ready, 1)
                    n = turn * U + j
                    if inside(n, PAIRS):
                        r, gslot, t0 = j % 2, (j // 2) % 4, (j % 2) * 2
                        act.wait_ge(x_in[gslot], turn * 32 + 32)
                        at_least(act, x_turned, n - 1)
                        act.activation(xH[:, r, :], flat(xs[:, gslot, t0:t0 + 2]), ACT.Copy).then_inc(xH_ready, 1)
                    n = turn * U + j - 5
                    if inside(n, PAIRS):
                        r = (j - 5) % 2
                        at_least(act, logits_done, 2 * n - 2)
                        act.wait_ge(y_turned, n + 1)
                        act.activation(yTH[:, r, :], bank[BTH][:, :], ACT.Copy)
                        act.activation(yTL[:, r, :], bank[BTL][:, :], ACT.Copy).then_inc(yT_ready, 1)
                    w_out(0)
                    n = turn * U + j - 7
                    if inside(n, PAIRS):
                        r = (j - 7) % 2
                        at_least(act, sums_in, n - 1)
                        act.wait_ge(w_ready, n + 1)
                        act.activation(wH[:, r, :], w[:, r, :], ACT.Copy).then_inc(wH_ready, 1)
                    w_out(1)
                    n = turn * U + j - 6
                    if inside(n, PAIRS):
                        r = (j - 6) % 2
                        act.wait_ge(shifted, 2 * n + 2)
                        act.activation(e[:, r, :], e[:, r, :], ACT.Exp).then_inc(exp_ready, 1)

                run_steps(act, PAIRS, LAG, U, 2, step)

            @block.tensor
            def _(pe):
                pe.wait_ge(ones_y, 3)
                for k in range(KC):
                    pe.matmul(bank[BS + k][:, :], zero_bf[:, 0:P], zero_bf[:, :], start=True, stop=False)

                def turn_parts(high, low):
                    for to, part in ((bank[BTH], high), (bank[BTL], low)):
                        for t in range(2):
                            for k in range(KC):
                                last = pe.transpose(to[:, t * D + k * P:t * D + (k + 1) * P].bitcast(F32R),
                                                    part(t, k), ident_r[:, :])
                    return last

                def step(turn, j):
                    n = turn * U + j - 1
                    if inside(n, PAIRS):
                        r = (j - 1) % 2
                        pe.wait_ge(xL_ready, n + 1)
                        at_least(pe, yT_ready, n - 4)
                        turn_parts(lambda t, k: xH[:, r, t * D + k * P:t * D + (k + 1) * P],
                                   lambda t, k: xL[:, r, t * D + k * P:t * D + (k + 1) * P]).then_inc(x_turned, 1)
                    n = turn * U + j - 6
                    if inside(n, PAIRS):
                        r = (j - 6) % 2
                        pe.wait_ge(yT_ready, n + 1)
                        for t in range(2):
                            at_least(pe, shifted, 2 * n + t - 1)
                            for k in range(KC):
                                at = slice(t * D + k * P, t * D + (k + 1) * P)
                                pe.matmul(bank[BL + t][:, :], yTH[:, r, at], CL[:, k, :], start=(k == 0), stop=False)
                                pe.matmul(bank[BL + t][:, :], yTL[:, r, at], CH[:, k, :], start=False, stop=False)
                                last = pe.matmul(bank[BL + t][:, :], yTH[:, r, at], CH[:, k, :], start=False,
                                                 stop=(k == KC - 1))
                            last.then_inc(logits_done, 1)
                    n = turn * U + j - 1
                    if inside(n, PAIRS):
                        r = (j - 1) % 2
                        pe.wait_ge(xT_ready, n + 1)
                        at_least(pe, z_ready, n)
                        for t in range(2):
                            to = bank[BZ][:, t * D:(t + 1) * D]
                            for k in range(KC):
                                at = slice(t * D + k * P, t * D + (k + 1) * P)
                                pe.matmul(to, xTH[:, r, at], W1L[:, k, :], start=(k == 0), stop=False)
                                pe.matmul(to, xTL[:, r, at], W1H[:, k, :], start=False, stop=False)
                                last = pe.matmul(to, xTH[:, r, at], W1H[:, k, :], start=False, stop=(k == KC - 1))
                        last.then_inc(z_done, 1)
                    n = turn * U + j - 5
                    if inside(n, PAIRS):
                        r = (j - 5) % 8
                        pe.wait_ge(yL_ready, n + 1)
                        at_least(pe, xT_ready, n + 5 if not isinstance(n, int) else min(n + 5, PAIRS))
                        turn_parts(lambda t, k: yH[:, r, t, k * (P + 1):k * (P + 1) + P],
                                   lambda t, k: yL[:, r, t, k * (P + 1):k * (P + 1) + P]).then_inc(y_turned, 1)
                    n = turn * U + j - 8
                    if inside(n, PAIRS):
                        r, ry = (j - 8) % 2, (j - 8) % 8
                        rows = LAST_ROWS if isinstance(n, int) and n >= PAIRS - 2 else P
                        pe.wait_ge(wL_ready, n + 1)
                        for t in range(2):
                            at_least(pe, wT_ready, 2 * n + t)
                            for k in range(HC):
                                to, at = bank[BW][:, k * P:(k + 1) * P], slice(t * HG + k * P, t * HG + (k + 1) * P)
                                pe.matmul(to, wH[:, r, at], ident_r[:, :], start=True, stop=False)
                                last = pe.matmul(to, wL[:, r, at], ident_r[:, :], start=False, stop=True)
                            last.then_inc(w_turned, 1)
                            all_w = slice(t * HG, (t + 1) * HG)
                            for k in range(KC):
                                at = slice(k * (P + 1), k * (P + 1) + P)
                                end = isinstance(n, int) and n == PAIRS - 1 and t == 1
                                pe.matmul(bank[BS + k][:, :], yH[0:rows, ry, t, at], wL[0:rows, r, all_w],
                                          start=False, stop=False)
                                pe.matmul(bank[BS + k][:, :], yL[0:rows, ry, t, at], wH[0:rows, r, all_w],
                                          start=False, stop=False)
                                last = pe.matmul(bank[BS + k][:, :], yH[0:rows, ry, t, at], wH[0:rows, r, all_w],
                                                 start=False, stop=end)
                        last.then_inc(sums_in, 1)

                run_steps(pe, PAIRS, LAG, U, 2, step)

        MH = sb("MH", [P, HC, D], F32R)
        ML = sb("ML", [P, HC, D], F32R)
        with ExitStack() as stage:
            zt = sb("zt", [P, KC, HG], stack=stage)
            norm_b = sb("norm_b", [P, HG], stack=stage)
            norm_r = sb("norm_r", [P, HG], stack=stage)
            tokT = sb("tokT", [HD, HG], stack=stage)
            qT = sb("qT", [HD, HG], stack=stage)
            kT = sb("kT", [HD, HG], stack=stage)
            val = sb("val", [HD, HG], stack=stage)
            amax = sb("amax", [HD, HEADS], stack=stage)
            att = sb("att", [HD, HG], stack=stage)
            asum = sb("asum", [HD, HEADS], stack=stage)
            arec = sb("arec", [HD, HEADS], stack=stage)
            attn = sb("attn", [HD, HG], stack=stage)
            attT = sb("attT", [HD, HG], stack=stage)
            oT = sb("oT", [HD, HG], stack=stage)
            M = sb("M", [P, HC, D], stack=stage)

            tv = sem("tokens_vector")
            tp = sem("tokens_tensor")
            ta = sem("tokens_scalar")
            wTg = sb("wTg", [P, SLOTS2, TILES * HG], stack=stage)
            x1g = sb("x1g", [P, SLOTS2, TILES * D], stack=stage)
            wTH = sb("wTH", [P, 2, TILES * HG], F32R, stack=stage)
            wTL = sb("wTL", [P, 2, TILES * HG], F32R, stack=stage)
            res = sb("res", [P, 2, TILES * D], stack=stage)

            w_in = [sem(f"w_in{i}") for i in range(SLOTS2)]
            high = sem("wTH_ready")
            low = sem("wTL_ready")
            mixed = sem("w_M_done")
            added = sem("res_ready")
            out_sent = [sem(f"out_sent{i}") for i in range(2)]
            wT_g = wT_s.rearrange("(g a) p n -> g p a n", a=2)

            block = stage.enter_context(nc.Block())

            def hs(h):
                return slice(h * HD, (h + 1) * HD)

            def by_head(ap):
                return ap.rearrange("p (h g) -> p h g", h=HEADS)

            @block.tensor
            def _(pe):
                pe.wait_ge(tv, 1)
                pe.matmul(bank[0][:, :], pick_last[:, :], zt[:, 1, :], start=True, stop=True).then_inc(tp, 1)
                for h in range(HEADS):
                    for k in range(KC):
                        last = pe.matmul(bank[1][0:HD, hs(h)], WfxA[:, k, hs(h)], zt[:, k, hs(h)],
                                         start=(k == 0), stop=(k == KC - 1))
                last.then_inc(tp, 1)
                pe.wait_ge(tv, 4)
                pe.matmul(bank[2][0:HD, :], wq[:, :], tokT[:, :], start=True, stop=True)
                pe.matmul(bank[3][0:HD, :], wk[:, :], tokT[:, :], start=True, stop=True)
                for h in range(HEADS):
                    last = pe.matmul(bank[4][0:HD, hs(h)], tokT[:, hs(h)], wv[:, :], start=True, stop=True)
                last.then_inc(tp, 1)
                pe.wait_ge(tv, 7)
                for h in range(HEADS):
                    last = pe.matmul(bank[5][0:HD, hs(h)], qT[:, hs(h)], kT[:, hs(h)], start=True, stop=True)
                last.then_inc(tp, 1)
                pe.wait_ge(tv, 12)
                for h in range(HEADS):
                    last = pe.transpose(bank[0][0:HD, hs(h)], attn[:, hs(h)], ident[0:HD, 0:HD])
                last.then_inc(tp, 1)
                pe.wait_ge(tv, 13)
                for h in range(HEADS):
                    last = pe.matmul(bank[1][0:HD, hs(h)], val[:, hs(h)], attT[:, hs(h)], start=True, stop=True)
                last.then_inc(tp, 1)
                pe.wait_ge(tv, 14)
                for h in range(HEADS):
                    last = pe.matmul(bank[2 + h // 2][:, (h % 2) * D:(h % 2 + 1) * D],
                                     oT[:, (h // 2) * P:(h // 2 + 1) * P], wo[:, h, :], start=True, stop=True)
                last.then_inc(tp, 1)

                def step(turn, j):
                    g = turn * SLOTS2 + j
                    if inside(g, GROUPS):
                        r = j % 2
                        pe.wait_ge(low, g + 1)
                        for q in range(2):
                            at_least(pe, added, 2 * g + q - 3)
                            for t in range(2):
                                to = bank[2 * r + q][:, t * D:(t + 1) * D]
                                for k in range(HC):
                                    at = slice(((q * 2 + t) * HC + k) * P, ((q * 2 + t) * HC + k + 1) * P)
                                    pe.matmul(to, wTH[:, r, at], ML[:, k, :], start=(k == 0), stop=False)
                                    pe.matmul(to, wTL[:, r, at], MH[:, k, :], start=False, stop=False)
                                    last = pe.matmul(to, wTH[:, r, at], MH[:, k, :], start=False,
                                                     stop=(k == HC - 1))
                            last.then_inc(mixed, 1)

                run_steps(pe, GROUPS, 0, SLOTS2, 1, step)

            @block.vector
            def _(v):
                done = [0]

                def then(instruction):
                    instruction.then_inc(tv, 1)
                    done[0] += 1
                    v.wait_ge(tv, done[0])

                v.tensor_copy(zt[:, 0, :], bank[6][:, :])
                then(v.tensor_copy(zt[:, 1, :], bank[7][:, :]))
                v.wait_ge(tp, 1)
                then(v.tensor_scalar(norm_b[:, :], bank[0][:, :], NORM_SHIFT, None, ALU.add))
                then(v.reciprocal(norm_r[:, :], norm_b[:, :]))
                v.wait_ge(tp, 2)
                then(v.tensor_tensor(tokT[:, :], bank[1][0:HD, :], norm_r[0:HD, :], ALU.mult))
                v.wait_ge(tp, 3)
                then(v.tensor_copy(qT[:, :], bank[2][0:HD, :]))
                then(v.tensor_copy(kT[:, :], bank[3][0:HD, :]))
                then(v.tensor_copy(val[:, :], bank[4][0:HD, :]))
                v.wait_ge(tp, 4)
                then(v.reduce_max(amax[:, :], by_head(bank[5][0:HD, :]), AX))
                then(v.tensor_tensor(by_head(att[:, :]), by_head(bank[5][0:HD, :]),
                                     amax[:, :].unsqueeze(2).to_broadcast([HD, HEADS, SLICES]), ALU.subtract))
                v.wait_ge(ta, 1)
                then(v.reduce_sum(asum[:, :], by_head(att[:, :]), AX))
                then(v.reciprocal(arec[:, :], asum[:, :]))
                then(v.tensor_tensor(by_head(attn[:, :]), by_head(att[:, :]),
                                     arec[:, :].unsqueeze(2).to_broadcast([HD, HEADS, SLICES]), ALU.mult))
                v.wait_ge(tp, 5)
                then(v.tensor_copy(attT[:, :], bank[0][0:HD, :]))
                v.wait_ge(tp, 6)
                then(v.tensor_copy(oT[:, :], bank[1][0:HD, :]))
                v.wait_ge(tp, 7)
                for h in range(HEADS):
                    half = slice((h % 2) * HD, (h % 2 + 1) * HD)
                    last = v.tensor_tensor(M[half, h // 2, :], bank[2 + h // 2][half, (h % 2) * D:(h % 2 + 1) * D],
                                           bo_part[half, :], ALU.add)
                then(last)
                then(v.tensor_copy(MH[:, :, :], M[:, :, :]))
                then(v.tensor_tensor(ML[:, :, :], M[:, :, :], MH[:, :, :].bitcast(F32), ALU.subtract))

                def step(turn, j):
                    g = turn * SLOTS2 + j
                    if inside(g, GROUPS):
                        at_least(v, mixed, 2 * g - 2)
                        v.wait_ge(high, g + 1)
                        v.tensor_tensor(wTL[:, j % 2, :], wTg[:, j, :], wTH[:, j % 2, :].bitcast(F32),
                                        ALU.subtract).then_inc(low, 1)
                    g = turn * SLOTS2 + j - 1
                    if inside(g, GROUPS):
                        r, x_slot = (j - 1) % 2, (j - 1) % SLOTS2
                        at_least(v, out_sent[r], (turn * (SLOTS2 // 2) + (j - 1) // 2) * 16)
                        for q in range(2):
                            v.wait_ge(mixed, 2 * g + q + 1)
                            v.tensor_tensor(res[:, r, q * 2 * D:(q + 1) * 2 * D], bank[2 * r + q][:, :],
                                            x1g[:, x_slot, q * 2 * D:(q + 1) * 2 * D], ALU.add).then_inc(added, 1)

                run_steps(v, GROUPS, 1, SLOTS2, 1, step)

            @block.scalar
            def _(act):
                act.wait_ge(tv, 9)
                act.activation(att[:, :], att[:, :], ACT.Exp, scale=SCALE).then_inc(ta, 1)

                def step(turn, j):
                    g = turn * SLOTS2 + j
                    if inside(g, GROUPS):
                        act.wait_ge(w_in[j], turn * 32 + 32)
                        at_least(act, mixed, 2 * g - 2)
                        act.activation(wTH[:, j % 2, :], wTg[:, j, :], ACT.Copy).then_inc(high, 1)

                run_steps(act, GROUPS, 0, SLOTS2, 1, step)

            @block.sync
            def _(sp):
                def step(turn, j):
                    g = turn * SLOTS2 + j
                    if inside(g, GROUPS):
                        at_least(sp, added, 2 * (g - SLOTS2 + 1))
                        sp.dma_start(wTg[:, j, :].rearrange("p (a n) -> p a n", a=2),
                                     wT_g[bass.ds(g, 1)].rearrange("g p a n -> (g p) a n")).then_inc(w_in[j], 16)
                        sp.dma_start(x1g[:, j, :], row(x1_g, g)).then_inc(w_in[j], 16)
                    g = turn * SLOTS2 + j - SLOTS2 + 1
                    if inside(g, GROUPS):
                        r = (j - SLOTS2 + 1) % 2
                        sp.wait_ge(added, 2 * g + 2)
                        if isinstance(g, int) and g == GROUPS - 1:
                            sp.dma_start(out_last, res[0:LAST_ROWS, r, :]).then_inc(out_sent[r], 16)
                        else:
                            sp.dma_start(row(out_g, g), res[:, r, :]).then_inc(out_sent[r], 16)

                run_steps(sp, GROUPS, SLOTS2 - 1, SLOTS2, 1, step)
                for i in range(2):
                    sp.wait_ge(out_sent[i], 16 * (GROUPS // 2))


_INS = ["x", "src", "dst", "L0_gnn_W", "L0_gnn_b", "L0_ffn_W_fx", "L0_ffn_b_fx", "L0_ffn_W_x", "L0_ffn_b_x",
        "L0_ffn_W_slice", "L0_ffn_b_slice", "L0_ffn_W_q", "L0_ffn_W_k", "L0_ffn_W_v", "L0_ffn_W_out",
        "L0_ffn_b_out", "L0_ffn_temperature"]


def kernel(**inputs):
    import numpy as _np
    import concourse.bacc as _bacc
    from concourse import mybir as _mybir
    from concourse.bass_utils import run_bass_kernel_spmd as _run

    nc = _bacc.Bacc("TRN2", target_bir_lowering=False, num_devices=1)
    arrays, args = {}, []
    for name in _INS:
        a = _np.ascontiguousarray(inputs[name])
        arrays[f"in_{name}"] = a
        args.append(nc.dram_tensor(f"in_{name}", a.shape, _mybir.dt.from_np(a.dtype), kind="ExternalInput").ap())
    result = nc.dram_tensor("out_x", (NODES, D), F32, kind="ExternalOutput").ap()
    build(nc, *args, result)
    r = _run(nc, [arrays], core_ids=[0])
    return r.results[0]["out_x"]
```
